# Optimizing a Trainium2 kernel written in Bass

```python
import numpy as np
import jax
import jax.numpy as jnp

def _softmax(x, axis=-1):
    return jax.nn.softmax(x, axis=axis)

def _gelu(x):
    return jax.nn.gelu(x, approximate=True)

def _silu(x):
    return jax.nn.silu(x)

def _sigmoid(x):
    return jax.nn.sigmoid(x)

def _layernorm(x, axis=-1, eps=1e-05):
    m = jnp.mean(x, axis=axis, keepdims=True)
    v = jnp.var(x, axis=axis, keepdims=True)
    return (x - m) / jnp.sqrt(v + eps)

def _scatter_add(tgt, idx, src, axis=0):
    return tgt.at[idx].add(src)

def _segment_sum(src, seg, n):
    return jax.ops.segment_sum(src, seg, n)
kernel_name = 'mk_prb_d1_jaxref_r4_63addc'

def setup_inputs(seed: int=0):
    np.random.seed(seed)
    _w = jnp.asarray

    def _L0_attn_setup():
        import jax, jax.numpy as jnp
        import numpy as np
        N_HEADS = 16
        ROPE_BASE = 10000.0

        def _rope(x):
            B, L, H, Dh = x.shape
            half = Dh // 2
            inv_freq = 1.0 / ROPE_BASE ** (jnp.arange(0, half, dtype=jnp.float32) / half)
            ang = jnp.arange(L, dtype=jnp.float32)[:, None] * inv_freq[None, :]
            cos = jnp.concatenate([jnp.cos(ang), jnp.cos(ang)], axis=-1).astype(x.dtype)
            sin = jnp.concatenate([jnp.sin(ang), jnp.sin(ang)], axis=-1).astype(x.dtype)
            cos = cos[None, :, None, :]
            sin = sin[None, :, None, :]
            x1, x2 = (x[..., :half], x[..., half:])
            rot = jnp.concatenate([-x2, x1], axis=-1)
            return x * cos + rot * sin
        key = jax.random.key(seed)
        k1, k2, k3 = jax.random.split(key, 3)
        B, L, D = (2, 512, 256)
        x = jax.random.normal(k1, (B, L, D), dtype=jnp.float32)
        w_qkv = jax.random.normal(k2, (3 * D, D), dtype=jnp.float32) * D ** (-0.5)
        w_out = jax.random.normal(k3, (D, D), dtype=jnp.float32) * D ** (-0.5)
        return {'x': x, 'w_qkv': w_qkv, 'w_out': w_out}
    _L0_attn_in = _L0_attn_setup()

    def _L0_ffn_setup():
        import jax, jax.numpy as jnp
        import numpy as np
        DIM = 256
        HIDDEN = 768
        SCALE = 1.0 / 127.0

        def _dequant(w_int, dtype):
            return w_int.astype(dtype) * jnp.asarray(SCALE, dtype)
        key = jax.random.key(seed)
        k_x, k_g, k_u, k_d = jax.random.split(key, 4)
        x = jax.random.normal(k_x, (4, 512, DIM), dtype=jnp.float32)
        w_gate = jax.random.randint(k_g, (HIDDEN, DIM), -127, 128, dtype=jnp.int32)
        w_up = jax.random.randint(k_u, (HIDDEN, DIM), -127, 128, dtype=jnp.int32)
        w_down = jax.random.randint(k_d, (DIM, HIDDEN), -127, 128, dtype=jnp.int32)
        return {'x': x, 'w_gate': w_gate, 'w_up': w_up, 'w_down': w_down}
    _L0_ffn_in = _L0_ffn_setup()
    _d = {'L0_attn_x': _L0_attn_in['x'], 'L0_attn_w_qkv': _L0_attn_in['w_qkv'], 'L0_attn_w_out': _L0_attn_in['w_out'], 'L0_ffn_w_gate': _L0_ffn_in['w_gate'], 'L0_ffn_w_up': _L0_ffn_in['w_up'], 'L0_ffn_w_down': _L0_ffn_in['w_down']}
    _x0 = _d['L0_attn_x']
    _d['L0_attn_x'] = jax.random.normal(jax.random.fold_in(jax.random.key(seed), 1), (4, 2048, 256), dtype=_x0.dtype)
    del _x0
    return _d

def reference(L0_attn_x, L0_attn_w_qkv, L0_attn_w_out, L0_ffn_w_gate, L0_ffn_w_up, L0_ffn_w_down):

    def _L0_attn_ref(x, w_qkv, w_out):
        import jax, jax.numpy as jnp
        import numpy as np
        N_HEADS = 16
        ROPE_BASE = 10000.0

        def _rope(x):
            B, L, H, Dh = x.shape
            half = Dh // 2
            inv_freq = 1.0 / ROPE_BASE ** (jnp.arange(0, half, dtype=jnp.float32) / half)
            ang = jnp.arange(L, dtype=jnp.float32)[:, None] * inv_freq[None, :]
            cos = jnp.concatenate([jnp.cos(ang), jnp.cos(ang)], axis=-1).astype(x.dtype)
            sin = jnp.concatenate([jnp.sin(ang), jnp.sin(ang)], axis=-1).astype(x.dtype)
            cos = cos[None, :, None, :]
            sin = sin[None, :, None, :]
            x1, x2 = (x[..., :half], x[..., half:])
            rot = jnp.concatenate([-x2, x1], axis=-1)
            return x * cos + rot * sin
        B, L, D = x.shape
        H = N_HEADS
        Dh = D // H
        qkv = jnp.einsum('bld,ed->ble', x, w_qkv)
        q, k, v = jnp.split(qkv, 3, axis=-1)
        q = q.reshape(B, L, H, Dh)
        k = k.reshape(B, L, H, Dh)
        v = v.reshape(B, L, H, Dh)
        q = _rope(q)
        k = _rope(k)
        scale = 1.0 / jnp.sqrt(jnp.asarray(Dh, dtype=x.dtype))
        scores = jnp.einsum('blhd,bmhd->bhlm', q, k) * scale
        attn = jax.nn.softmax(scores, axis=-1)
        out = jnp.einsum('bhlm,bmhd->blhd', attn, v).reshape(B, L, D)
        return jnp.einsum('bld,ed->ble', out, w_out)

    def _L0_ffn_ref(x, w_gate, w_up, w_down):
        import jax, jax.numpy as jnp
        import numpy as np
        DIM = 256
        HIDDEN = 768
        SCALE = 1.0 / 127.0

        def _dequant(w_int, dtype):
            return w_int.astype(dtype) * jnp.asarray(SCALE, dtype)
        wg = _dequant(w_gate, x.dtype)
        wu = _dequant(w_up, x.dtype)
        wd = _dequant(w_down, x.dtype)
        gate = jnp.einsum('bsd,hd->bsh', x, wg)
        up = jnp.einsum('bsd,hd->bsh', x, wu)
        h = jax.nn.silu(gate) * up
        return jnp.einsum('bsh,dh->bsd', h, wd)
    x = L0_attn_x
    xn = _layernorm(x, axis=-1)
    x = x + _L0_attn_ref(xn, L0_attn_w_qkv, L0_attn_w_out) + _L0_ffn_ref(xn, L0_ffn_w_gate, L0_ffn_w_up, L0_ffn_w_down)
    return x

_drawn_inputs = setup_inputs


def setup_inputs(seed=0):
    import zlib

    import numpy as np

    out = dict(_drawn_inputs(seed))
    spreads = {}
    factors = {'L0_attn_w_qkv': 8.0, 'L0_attn_w_out': 8.0}
    for name, (base, spread) in spreads.items():
        noise = np.random.default_rng([zlib.crc32(name.encode()), seed]).standard_normal(out[name].shape)
        drawn = base * np.exp(spread * noise) if base else spread * noise
        out[name] = jnp.asarray(drawn.astype(out[name].dtype))
    for name, factor in factors.items():
        out[name] = (out[name] * factor).astype(out[name].dtype)
    return out
```

```python
from contextlib import ExitStack

import concourse.bass as bass
from concourse import mybir

F32 = mybir.dt.float32
BF16 = mybir.dt.bfloat16
I32 = mybir.dt.int32
ALU = mybir.AluOpType
ACT = mybir.ActivationFunctionType
AX = mybir.AxisListType

P = 128
DH = 16
BANK = 512
TILES = 16
BLK = 4
PARTS = 3
Q_PART = [0, 1, 2, 0, 1, 0]
K_PART = [0, 0, 0, 1, 1, 2]
ROWS = len(Q_PART) * DH
SLOTS = 4
LAG = 3
RING = 3
UNROLL = SLOTS * TILES
EPS = 1e-5
QUANT_SCALE = 1.0 / 127.0


def layer_program(nc, x, w_qkv, w_out, w_gate, w_up, w_down, cos_tab, sin_tab, ident_in, out, y_dram, qk_dram):
    TOKENS, D = x.shape
    HID = w_gate.shape[0]
    H = D // DH
    KT = D // P
    HT = HID // P
    NT = TOKENS // P
    NBLK = NT // BLK
    HEADS = (TOKENS // (TILES * P)) * H
    SCALE = float(DH) ** -0.5
    assert D == 256 and KT == 2 and HEADS % SLOTS == 0

    x_blocks = x.rearrange("(k t p) d -> k p t d", p=P, t=BLK)
    y_blocks = y_dram.rearrange("(k t p) d -> k p t d", p=P, t=BLK)
    out_blocks = out.rearrange("(k t p) d -> k p t d", p=P, t=BLK)

    keep = ExitStack()

    def sb(stack, name, shape, dt=F32):
        return stack.enter_context(nc.sbuf_tensor(name, shape, dt))

    def sem(name):
        return keep.enter_context(nc.semaphore(name))

    ident = sb(keep, "ident", [P, P])
    ident16 = sb(keep, "ident16", [P, P], BF16)
    v_space = sb(keep, "v_space", [P, max(NT * D, (3 * D * D + 3 * 2 * HID * D + D * D) // P)])
    v_all = v_space[:, 0:NT * D].rearrange("p (t h d) -> p t h d", h=H, d=DH)
    woT = sb(keep, "woT", [P, KT, D])
    sa = ExitStack()
    wT = sb(sa, "wT", [P, 3 * KT * D + 2 * KT * HID + HT * D])
    o0 = 0
    wqkvT = wT[:, o0:o0 + KT * 3 * D].rearrange("p (k e) -> p k e", k=KT)
    o0 += KT * 3 * D
    wgT = wT[:, o0:o0 + KT * HID].rearrange("p (k e) -> p k e", k=KT)
    o0 += KT * HID
    wuT = wT[:, o0:o0 + KT * HID].rearrange("p (k e) -> p k e", k=KT)
    o0 += KT * HID
    wdT = wT[:, o0:o0 + HT * D].rearrange("p (k e) -> p k e", k=HT)

    cos_t = sb(sa, "cos_t", [P, NT, DH // 2])
    sin_t = sb(sa, "sin_t", [P, NT, DH])
    x_ln = sb(sa, "x_ln", [P, BLK, D])
    x_res = sb(sa, "x_res", [P, BLK, D])
    stats = sb(sa, "stats", [P, BLK, 6])
    mv = sb(sa, "mv", [P, BLK, 2])
    ve = sb(sa, "ve", [P, BLK])
    seed = sb(sa, "seed", [P, BLK], I32)
    rs = sb(sa, "rs", [P, 4, BLK])
    nt_a = sb(sa, "nt_a", [P, 3, BLK])
    nt_b = sb(sa, "nt_b", [P, 3, BLK])
    xn = sb(sa, "xn", [P, BLK, D])
    xnT = sb(sa, "xnT", [P, KT, BLK * P])
    rot_c = sb(sa, "rot_c", [P, 2, 2 * D])
    rot_s = sb(sa, "rot_s", [P, 2, 2 * D])
    qk_rot = sb(sa, "qk_rot", [P, 2, 2 * D])
    qk_rem = sb(sa, "qk_rem", [P, 2, 2 * D])
    parts = sb(sa, "parts", [P, 2, PARTS, 2 * D], BF16)
    staged = sb(sa, "staged", [P, PARTS, 2 * KT, BLK * P], BF16)
    silu = sb(sa, "silu", [P, 2, BANK])
    hT = sb(sa, "hT", [P, HT, BLK * P])
    y_blk = sb(sa, "y_blk", [P, BLK, D])
    n0 = 0
    nat = {}
    for nm, rows, cols in (("qkv", 3 * D, D), ("g", HID, D), ("u", HID, D), ("o", D, D), ("d", D, HID),
                           ("gi", HID, D), ("ui", HID, D), ("di", D, HID)):
        n = rows // P * cols
        nat[nm] = v_space[:, n0:n0 + n]
        if nm.endswith("i"):
            nat[nm] = nat[nm].bitcast(I32)
        nat[nm] = nat[nm].rearrange("p (t c) -> p t c", c=cols)
        n0 += n
    sa.close()

    sB = ExitStack()
    o_all = sb(sB, "o_all", [P, NT, H, DH])
    q_op = sb(sB, "q_op", [P, SLOTS, TILES * P], BF16)
    k_op = sb(sB, "k_op", [P, SLOTS, TILES * P], BF16)
    probs = sb(sB, "probs", [P, 2, TILES * P])
    v_op = sb(sB, "v_op", [P, 2, TILES, 32])
    row_max = sb(sB, "row_max", [P, 2, TILES, 2])
    neg_max = sb(sB, "neg_max", [P, TILES])
    neg_rem = sb(sB, "neg_rem", [P, TILES])
    stab = sb(sB, "stab", [P, P // TILES, TILES], BF16)
    stabT = sb(sB, "stabT", [PARTS * TILES, P], BF16)
    acc_sb = sb(sB, "acc_sb", [P, BANK])
    oT_sb = sb(sB, "oT_sb", [P, BANK])
    inv_sum = sb(sB, "inv_sum", [P, 4, 4])
    sB.close()
    n_c = BLK * D
    o_blk, oT, y_in, res = (v_space[:, 2 * n * n_c:2 * (n + 1) * n_c] for n in range(4))
    o_blk, y_in, res = (a.rearrange("p (j t d) -> p j t d", j=2, t=BLK) for a in (o_blk, y_in, res))
    oT = oT.rearrange("p (j k n) -> p j k n", j=2, k=KT)

    psum = keep.enter_context(nc.psum_tensor("psum", [P, 8 * BANK], F32))

    def bank(n, cols=BANK):
        return psum[:, n * BANK:n * BANK + cols]

    w_loaded = sem("w_loaded")
    ident_loaded = sem("ident_loaded")
    tables_loaded = sem("tables_loaded")
    ident16_ready = sem("ident16_ready")
    w_scaled = sem("w_scaled")
    wt_full = sem("wt_full")
    wt_saved = sem("wt_saved")
    x_loaded = sem("x_loaded")
    xres_loaded = sem("xres_loaded")
    ln_step = sem("ln_step")
    xn_ready = sem("xn_ready")
    xT_full = sem("xT_full")
    xT_saved = sem("xT_saved")
    pair_full = sem("pair_full")
    pair_used = sem("pair_used")
    silu_ready = sem("silu_ready")
    rope_ready = sem("rope_ready")
    qk_ready = sem("qk_ready")
    split_step = sem("split_step")
    parts_ready = sem("parts_ready")
    partsT_full = sem("partsT_full")
    partsT_saved = sem("partsT_saved")
    staged_out = sem("staged_out")
    down_full = sem("down_full")
    y_ready = sem("y_ready")
    y_out = sem("y_out")
    b_const = sem("b_const")
    qk_loaded = [sem(f"qk_loaded{s}") for s in range(SLOTS)]
    stab_loaded = sem("stab_loaded")
    s1_full = sem("s1_full")
    s1_used = sem("s1_used")
    s2_full = sem("s2_full")
    s2_used = sem("s2_used")
    pv_done = sem("pv_done")
    acc_saved = sem("acc_saved")
    v_ready = sem("v_ready")
    stab_step = sem("stab_step")
    sum_inv = sem("sum_inv")
    o_ready = sem("o_ready")
    c_gathered = sem("c_gathered")
    cT_full = sem("cT_full")
    cT_saved = sem("cT_saved")
    proj_full = sem("proj_full")
    yin_loaded = [sem("yin_loaded0"), sem("yin_loaded1")]
    res_ready = sem("res_ready")
    res_out = [sem("res_out0"), sem("res_out1")]

    wt_blocks = ([("o", j, k) for k in range(KT) for j in range(D // P)]
                 + [("qkv", j, k) for k in range(KT) for j in range(3 * D // P)]
                 + [("g", j, k) for k in range(KT) for j in range(HT)]
                 + [("u", j, k) for k in range(KT) for j in range(HT)]
                 + [("d", j, k) for k in range(HT) for j in range(D // P)])
    WG = len(wt_blocks) // 4

    PAIRS = BLK + HT
    LN_STEPS = 5 + 3 * 4
    N_STAGED = 2 * KT

    N1 = HEADS * TILES
    FIRST2 = TILES + LAG
    STAB_AT = TILES + 1
    SAVE_AT = FIRST2 + TILES + 1
    TURN_AT = SAVE_AT + 1
    NORM_AT = TURN_AT + 1
    VCOPY_AT = 10
    STEPS_B = N1 + (NORM_AT - TILES) + 1
    HEAD_ITEMS = 4 * TILES + 2
    assert HEAD_ITEMS % RING == 0
    PRO = NORM_AT
    BODIES = (N1 - PRO) // UNROLL

    def head_of(g, at):
        h, r = divmod(g - at, TILES)
        return h if r == 0 and 0 <= h < HEADS else None

    def sequence_of(h):
        n = h >> (H.bit_length() - 1)
        if not isinstance(h, int):
            n.max_val = HEADS // H - 1
        return n

    def before(g, at):
        return min(max((g - at + TILES - 1) // TILES, 0), HEADS)

    def items_before(g):
        return 4 * min(max(g - FIRST2, 0), N1) + before(g, STAB_AT) + before(g, TURN_AT)

    def extra_items(g):
        return (head_of(g, STAB_AT) is not None) + (head_of(g, TURN_AT) is not None)

    def run_steps(eng, step):
        for c in range(PRO):
            step(c, 0)
        if BODIES:
            with eng.Fori(0, BODIES) as i:
                for c in range(PRO, PRO + UNROLL):
                    step(c, i)
        for c in range(PRO + UNROLL * BODIES, STEPS_B):
            step(c, 0)

    block = keep.enter_context(nc.Block())

    @block.sync
    def _(sp):
        sp.dma_start(ident[:, :], ident_in).then_inc(ident_loaded, 16)
        sp.dma_start(nat["qkv"], w_qkv.rearrange("(t p) c -> p t c", p=P)).then_inc(w_loaded, 16)
        sp.dma_start(nat["o"], w_out.rearrange("(t p) c -> p t c", p=P)).then_inc(w_loaded, 16)
        sp.dma_start(nat["gi"], w_gate.rearrange("(t p) c -> p t c", p=P)).then_inc(w_loaded, 16)
        sp.dma_start(nat["ui"], w_up.rearrange("(t p) c -> p t c", p=P)).then_inc(w_loaded, 16)
        sp.dma_start(nat["di"], w_down.rearrange("(t p) c -> p t c", p=P)).then_inc(w_loaded, 16)
        sp.dma_start(x_ln[:, :, :], x_blocks[0]).then_inc(x_loaded, 16)
        sp.dma_start(cos_t[:, :, :], cos_tab).then_inc(tables_loaded, 16)
        sp.dma_start(sin_t[:, :, :], sin_tab).then_inc(tables_loaded, 16)

        def block_a(k, last):
            if not (isinstance(k, int) and k == 0):
                sp.wait_ge(y_ready, BLK * k)
            sp.dma_start(x_res[:, :, :], x_blocks[k]).then_inc(xres_loaded, 16)
            if not last:
                sp.wait_ge(xn_ready, k + 1)
                sp.dma_start(x_ln[:, :, :], x_blocks[k + 1]).then_inc(x_loaded, 16)
            sp.wait_ge(partsT_saved, BLK * (k + 1))
            for qg in range(2 * KT):
                dst = qk_dram[qg // KT, :, (qg % KT) * P:(qg % KT + 1) * P, bass.ds(k * (BLK * P), BLK * P)]
                sp.dma_start(dst.rearrange("a r n -> r a n"), staged[:, :, qg, :]).then_inc(staged_out, 16)
            sp.wait_ge(y_ready, BLK * (k + 1))
            sp.dma_start(y_blocks[k], y_blk[:, :, :]).then_inc(y_out, 16)

        block_a(0, False)
        with sp.Fori(1, NBLK - 1) as k:
            block_a(k, False)
        block_a(NBLK - 1, True)

        sp.wait_ge(staged_out, 16 * N_STAGED * NBLK)
        sp.wait_ge(y_out, 16 * NBLK)
        sp.wait_ge(down_full, BLK * NBLK)

        def load_head(hl, i):
            h = hl + SLOTS * i
            s = hl % SLOTS
            head = (h & (H - 1)) * DH
            tok = sequence_of(h) * (TILES * P)
            src = qk_dram[:, :, bass.ds(head, DH), bass.ds(tok, TILES * P)]
            r = 0
            for n in (3, 2, 1):
                sp.dma_start(q_op[r * DH:(r + n) * DH, s, :], src[0, 0:n]).then_inc(qk_loaded[s], 16)
                r += n
            for r in range(len(K_PART)):
                sp.dma_start(k_op[r * DH:(r + 1) * DH, s, :], src[1, K_PART[r]]).then_inc(qk_loaded[s], 16)

        def load_stab(hl, i):
            h = hl + SLOTS * i
            g = TILES * hl + STAB_AT
            sp.wait_ge(s2_used, items_before(g) + 1 + HEAD_ITEMS * SLOTS * i)
            dst = q_op[ROWS:ROWS + PARTS, hl % SLOTS, :].rearrange("a (t n) -> a t n", t=TILES)
            sp.dma_start(dst, stabT[:, :]).then_inc(stab_loaded, 16)

        load_head(0, 0)
        load_head(1, 0)
        for hl in range(SLOTS):
            load_stab(hl, 0)
            load_head(hl + 2, 0)
        with sp.Fori(0, HEADS // SLOTS - 2) as i:
            for hl in range(SLOTS, 2 * SLOTS):
                load_stab(hl, i)
                load_head(hl + 2, i)
        for hl in range(HEADS - SLOTS, HEADS):
            load_stab(hl, 0)
            if hl + 2 < HEADS:
                load_head(hl + 2, 0)

        sp.wait_ge(o_ready, HEADS)

        def load_y(n, j):
            sp.dma_start(y_in[:, j], y_blocks[2 * n + j]).then_inc(yin_loaded[j], 16)

        def store_out(n, j):
            sp.wait_ge(res_ready, 2 * (2 * n + j + 1))
            sp.dma_start(out_blocks[2 * n + j], res[:, j]).then_inc(res_out[j], 16)

        for j in range(2):
            load_y(0, j)
        with sp.Fori(0, NBLK // 2 - 1) as n:
            for j in range(2):
                store_out(n, j)
                load_y(n + 1, j)
        for j in range(2):
            store_out(NBLK // 2 - 1, j)
        for j in range(2):
            sp.wait_ge(res_out[j], 16 * (NBLK // 2))

    @block.tensor
    def _(pe):
        pe.wait_ge(ident_loaded, 16)
        pe.wait_ge(w_scaled, 3)
        pe.wait_ge(w_loaded, 80)
        for grp in range(WG):
            if grp >= 4:
                pe.wait_ge(wt_saved, grp - 3)
            for j in range(4):
                nm, r, c = wt_blocks[4 * grp + j]
                mm = pe.transpose(bank(grp % 4)[:, j * P:(j + 1) * P], nat[nm][:, r, c * P:(c + 1) * P], ident[:, :])
            mm.then_inc(wt_full, 1)
        pe.wait_ge(wt_saved, WG)
        pe.wait_ge(ident16_ready, 1)

        def block_a(k):
            pe.wait_ge(xn_ready, k + 1)
            if not (isinstance(k, int) and k == 0):
                pe.wait_ge(partsT_saved, BLK * k)
            for c in range(KT):
                for t in range(BLK):
                    mm = pe.transpose(bank(c)[:, t * P:(t + 1) * P], xn[:, t, c * P:(c + 1) * P], ident[:, :])
                mm.then_inc(xT_full, 1)

            def take_pair(u, k):
                if u >= 2 or not isinstance(k, int):
                    pe.wait_ge(pair_used, PAIRS * k + u - 1)
                elif k > 0:
                    pe.wait_ge(pair_used, PAIRS * k + u - 1)

            for t in range(BLK):
                if t == 0:
                    pe.wait_ge(xT_saved, KT * (k + 1))
                take_pair(t, k) if not (isinstance(k, int) and k == 0 and t < 2) else None
                a, b = 2 + 2 * (t % 2), 3 + 2 * (t % 2)
                for c in range(KT):
                    pe.matmul(bank(a), xnT[:, c, t * P:(t + 1) * P], wqkvT[:, c, 0:2 * D], start=(c == 0), stop=(c == KT - 1))
                for c in range(KT):
                    mm = pe.matmul(bank(b, D), xnT[:, c, t * P:(t + 1) * P], wqkvT[:, c, 2 * D:3 * D],
                                   start=(c == 0), stop=(c == KT - 1))
                mm.then_inc(pair_full, 1)
            for j in range(HT):
                take_pair(BLK + j, k)
                a, b = 2 + 2 * (j % 2), 3 + 2 * (j % 2)
                for w, dst in ((wgT, a), (wuT, b)):
                    for c in range(KT):
                        mm = pe.matmul(bank(dst), w[:, c, j * P:(j + 1) * P], xnT[:, c, :], start=(c == 0), stop=(c == KT - 1))
                mm.then_inc(pair_full, 1)
                if j < BLK:
                    pe.wait_ge(parts_ready, BLK * k + j + 1)
                    if j == 0:
                        pe.wait_ge(xT_saved, KT * (k + 1))
                    else:
                        pe.wait_ge(partsT_saved, BLK * k + j)
                    turned = psum[:, 0:2 * BANK].bitcast(BF16)
                    for n in range(PARTS * 2 * KT):
                        a, qg = divmod(n, 2 * KT)
                        mm = pe.transpose(turned[:, n * P:(n + 1) * P], parts[:, j % 2, a, qg * P:(qg + 1) * P], ident16[:, :])
                    mm.then_inc(partsT_full, 1)
            for t in range(BLK):
                if t == 0:
                    pe.wait_ge(pair_used, PAIRS * (k + 1))
                if t >= 2 or not (isinstance(k, int) and k == 0):
                    pe.wait_ge(y_ready, BLK * k + t - 1)
                for j in range(HT):
                    mm = pe.matmul(bank(6 + t % 2, D), hT[:, j, t * P:(t + 1) * P], wdT[:, j, :],
                                   start=(j == 0), stop=(j == HT - 1))
                mm.then_inc(down_full, 1)

        block_a(0)
        with pe.Fori(1, NBLK) as k:
            block_a(k)

        pe.wait_ge(b_const, 4)
        pe.wait_ge(y_ready, BLK * NBLK)
        pe.wait_ge(partsT_saved, BLK * NBLK)

        def max_half(c, i, half):
            hl, t = divmod(c, TILES)
            if t == 0 and half == 0:
                nd = 16 * (3 + len(K_PART))
                pe.wait_ge(qk_loaded[hl % SLOTS], nd * (hl // SLOTS + 1 + i))
            n = 2 * c + half
            if n >= 2:
                pe.wait_ge(s1_used, n - 1 + 2 * UNROLL * i)
            s = hl % SLOTS
            for j in range(2):
                cols = (2 * half + j) * BANK
                mm = pe.matmul(bank(2 * half + j), q_op[0:ROWS, s, t * P:(t + 1) * P], k_op[0:ROWS, s, cols:cols + BANK],
                               start=True, stop=True)
            mm.then_inc(s1_full, 1)

        def step(c, i):
            item = items_before(c)

            def take_bank(item):
                if item >= RING:
                    pe.wait_ge(s2_used, item - RING + 1 + HEAD_ITEMS * SLOTS * i)
                return 4 + item % RING

            if c < N1:
                max_half(c, i, 0)
            h = head_of(c, STAB_AT)
            if h is not None:
                pe.wait_ge(stab_step, 5 * (h + 1 + SLOTS * i))
                b = take_bank(item)
                pe.transpose(bank(b).bitcast(BF16)[:, 0:P], stab[:, :, :].rearrange("p a t -> p (a t)"),
                             ident16[:, :]).then_inc(s2_full, 1)
                item += 1
            h = head_of(c, TURN_AT)
            if h is not None:
                pe.wait_ge(acc_saved, h + 1 + SLOTS * i)
                b = take_bank(item)
                for n in range(4):
                    mm = pe.transpose(bank(b)[:, n * P:(n + 1) * P], acc_sb[:, n * P:(n + 1) * P], ident[:, :])
                mm.then_inc(s2_full, 1)
                item += 1
            g2 = c - FIRST2
            for j in range(4):
                if j == 2 and c < N1:
                    max_half(c, i, 1)
                if 0 <= g2 < N1:
                    h, t = divmod(g2, TILES)
                    if t == 0 and j == 0:
                        pe.wait_ge(stab_loaded, 16 * (h + 1 + SLOTS * i))
                    b = take_bank(item)
                    pe.matmul(bank(b), k_op[0:ROWS + PARTS, h % SLOTS, t * P:(t + 1) * P],
                              q_op[0:ROWS + PARTS, h % SLOTS, j * BANK:(j + 1) * BANK],
                              start=True, stop=True).then_inc(s2_full, 1)
                    item += 1
            g3 = g2 - 1
            if 0 <= g3 < N1:
                h, t = divmod(g3, TILES)
                if t == 0:
                    pe.wait_ge(v_ready, h + 1 + SLOTS * i)
                    if h >= 1:
                        pe.wait_ge(acc_saved, h + SLOTS * i)
                pe.wait_ge(s2_used, items_before(c - 1) + extra_items(c - 1) + 4 + HEAD_ITEMS * SLOTS * i)
                for j in range(4):
                    mm = pe.matmul(bank(7)[32 * j:32 * j + 32, :], v_op[:, h % 2, t, :], probs[:, g3 % 2, j * BANK:(j + 1) * BANK],
                                   start=(t == 0), stop=(t == TILES - 1), tile_position=(0, 32 * j))
                mm.then_inc(pv_done, 1)

        run_steps(pe, step)

        def block_c(n, j, first):
            k = 2 * n + j
            pe.wait_ge(c_gathered, k + 1)
            if not first:
                pe.wait_ge(cT_saved, KT * (k - 1))
            for c in range(KT):
                for t in range(BLK):
                    mm = pe.transpose(bank(2 * j + c)[:, t * P:(t + 1) * P], o_blk[:, j, t, c * P:(c + 1) * P], ident[:, :])
                mm.then_inc(cT_full, 1)

        def block_c2(n, j, first):
            k = 2 * n + j
            pe.wait_ge(cT_saved, KT * (k + 1))
            if not first:
                pe.wait_ge(res_ready, 2 * (k - 1))
            for t in range(BLK):
                for c in range(KT):
                    mm = pe.matmul(psum[:, (4 + 2 * j) * BANK + t * D:(4 + 2 * j) * BANK + (t + 1) * D],
                                   oT[:, j, c, t * P:(t + 1) * P], woT[:, c, :], start=(c == 0), stop=(c == KT - 1))
                if t % 2 == 1:
                    mm.then_inc(proj_full, 1)

        pe.wait_ge(s1_used, 2 * N1)
        pe.wait_ge(s2_used, items_before(STEPS_B))
        for j in range(2):
            block_c(0, j, True)
        for j in range(2):
            block_c2(0, j, True)
        with pe.Fori(1, NBLK // 2) as n:
            for j in range(2):
                block_c(n, j, False)
            for j in range(2):
                block_c2(n, j, False)

    @block.scalar
    def _(act):
        for grp in range(WG):
            act.wait_ge(wt_full, grp + 1)
            dst = woT[:, :, :].rearrange("p k e -> p (k e)") if grp == 0 else wT[:, (grp - 1) * BANK:grp * BANK]
            nc.scalar.activation(dst, bank(grp % 4), ACT.Copy).then_inc(wt_saved, 1)

        def block_a(k):
            for c in range(KT):
                act.wait_ge(xT_full, KT * k + c + 1)
                nc.scalar.activation(xnT[:, c, :], bank(c), ACT.Copy).then_inc(xT_saved, 1)
            for j in range(HT):
                act.wait_ge(pair_full, PAIRS * k + BLK + j + 1)
                nc.scalar.activation(silu[:, j % 2, :], bank(2 + 2 * (j % 2)), ACT.Silu).then_inc(silu_ready, 1)
                if j < BLK:
                    if j == 0 and not (isinstance(k, int) and k == 0):
                        act.wait_ge(staged_out, 16 * N_STAGED * k)
                    act.wait_ge(partsT_full, BLK * k + j + 1)
                    nc.scalar.activation(staged[:, :, :, j * P:(j + 1) * P],
                                         psum[:, 0:2 * BANK].bitcast(BF16)[:, 0:PARTS * 2 * KT * P].rearrange(
                                             "p (a q n) -> p a q n", a=PARTS, q=2 * KT),
                                         ACT.Copy).then_inc(partsT_saved, 1)

        block_a(0)
        with act.Fori(1, NBLK) as k:
            block_a(k)

        act.wait_ge(down_full, BLK * NBLK)
        act.wait_ge(y_ready, BLK * NBLK)
        act.wait_ge(y_out, 16 * NBLK)
        act.wait_ge(staged_out, 16 * N_STAGED * NBLK)

        def step(c, i):
            item = items_before(c)

            def arrived(item):
                act.wait_ge(s2_full, item + 1 + HEAD_ITEMS * SLOTS * i)
                return 4 + item % RING

            h = head_of(c, SAVE_AT)
            if h is not None:
                act.wait_ge(pv_done, TILES * (h + 1 + SLOTS * i))
                nc.scalar.activation(acc_sb[:, :], bank(7), ACT.Copy).then_inc(acc_saved, 1)
            h = head_of(c, STAB_AT)
            if h is not None:
                if h >= 1:
                    act.wait_ge(stab_loaded, 16 * (h + SLOTS * i))
                b = arrived(item)
                nc.scalar.activation(stabT[:, :], bank(b).bitcast(BF16)[0:PARTS * TILES, 0:P], ACT.Copy).then_inc(s2_used, 1)
                item += 1
            h = head_of(c, TURN_AT)
            if h is not None:
                if h >= 1:
                    act.wait_ge(o_ready, h + SLOTS * i)
                b = arrived(item)
                nc.scalar.activation(oT_sb[:, :], bank(b), ACT.Copy).then_inc(s2_used, 1)
                item += 1
            g2 = c - FIRST2
            if 0 <= g2 < N1:
                if g2 >= 2:
                    act.wait_ge(pv_done, g2 - 1 + UNROLL * i)
                for j in range(4):
                    b = arrived(item)
                    nc.scalar.activation(probs[:, g2 % 2, j * BANK:(j + 1) * BANK], bank(b), ACT.Exp,
                                         scale=SCALE).then_inc(s2_used, 1)
                    item += 1

        run_steps(act, step)

        def block_c(n, j, first):
            k = 2 * n + j
            if not first:
                act.wait_ge(proj_full, 2 * (k - 1))
            for c in range(KT):
                act.wait_ge(cT_full, KT * k + c + 1)
                nc.scalar.activation(oT[:, j, c, :], bank(2 * j + c), ACT.Copy).then_inc(cT_saved, 1)

        for j in range(2):
            block_c(0, j, True)
        with act.Fori(1, NBLK // 2) as n:
            for j in range(2):
                block_c(n, j, False)

    @block.gpsimd
    def _(pool):
        pool.wait_ge(ident_loaded, 16)
        nc.gpsimd.tensor_copy(ident16[:, :], ident[:, :]).then_inc(ident16_ready, 1)

        def block_a(k):
            for t in range(BLK):
                pool.wait_ge(rope_ready, BLK * k + t + 1)
                nc.gpsimd.tensor_tensor(qk_rot[:, t % 2, :], rot_c[:, t % 2, :], rot_s[:, t % 2, :],
                                        ALU.add).then_inc(qk_ready, 1)

        with pool.Fori(0, NBLK) as k:
            block_a(k)

        pool.wait_ge(down_full, BLK * NBLK)
        pool.wait_ge(y_ready, BLK * NBLK)
        pool.wait_ge(y_out, 16 * NBLK)
        pool.wait_ge(staged_out, 16 * N_STAGED * NBLK)
        nc.gpsimd.memset(k_op[ROWS:ROWS + 32, :, :], 1.0).then_inc(b_const, 1)
        pool.wait_ge(b_const, 1)
        nc.gpsimd.memset(v_op[:, :, :, DH:DH + 1], 1.0).then_inc(b_const, 1)
        pool.wait_ge(b_const, 2)
        nc.gpsimd.memset(v_op[:, :, :, DH + 1:32], 0.0).then_inc(b_const, 1)
        pool.wait_ge(b_const, 3)
        nc.gpsimd.memset(stab[:, :, :], 0.0).then_inc(b_const, 1)

    @block.vector
    def _(dve):
        dve.wait_ge(w_loaded, 80)
        nc.vector.tensor_scalar(nat["g"], nat["gi"], QUANT_SCALE, None, ALU.mult).then_inc(w_scaled, 1)
        nc.vector.tensor_scalar(nat["u"], nat["ui"], QUANT_SCALE, None, ALU.mult).then_inc(w_scaled, 1)
        nc.vector.tensor_scalar(nat["d"], nat["di"], QUANT_SCALE, None, ALU.mult).then_inc(w_scaled, 1)

        def row_stats(k):
            dve.wait_ge(x_loaded, 16 * (k + 1))
            for t in range(BLK):
                ins = nc.vector.bn_stats(stats[:, t, :], x_ln[:, t, :])
            ins.then_inc(ln_step, 1)
            dve.wait_ge(ln_step, LN_STEPS * k + 1)

        def layer_norm(k, first):
            n = [LN_STEPS * k + 1]

            def done(ins):
                n[0] = n[0] + 1
                ins.then_inc(ln_step, 1)

            def wait():
                dve.wait_ge(ln_step, n[0])

            for t in range(BLK):
                ins = nc.vector.bn_aggr(mv[:, t, :], stats[:, t, :])
            done(ins)
            wait()
            done(nc.vector.tensor_scalar(ve[:, :], mv[:, :, 1], EPS, None, ALU.add))
            wait()
            done(nc.vector.tensor_scalar(seed[:, :], ve[:, :].bitcast(I32), 1, None, ALU.logical_shift_right))
            wait()
            done(nc.vector.tensor_scalar(rs[:, 0, :].bitcast(I32), seed[:, :], -1.0, float(0x5F3759DF), ALU.mult, ALU.add))
            for r in range(3):
                wait()
                done(nc.vector.tensor_tensor(nt_a[:, r, :], rs[:, r, :], rs[:, r, :], ALU.mult))
                wait()
                done(nc.vector.tensor_tensor(nt_b[:, r, :], nt_a[:, r, :], ve[:, :], ALU.mult))
                wait()
                dst = nt_a[:, r, :]
                done(nc.vector.tensor_scalar(dst, nt_b[:, r, :], -0.5, 1.5, ALU.mult, ALU.add))
                wait()
                if r < 2:
                    done(nc.vector.tensor_tensor(rs[:, r + 1, :], rs[:, r, :], dst, ALU.mult))
                else:
                    nc.vector.tensor_tensor(rs[:, r + 1, :], rs[:, r, :], dst, ALU.mult).then_inc(ln_step, 1)
                    n[0] = n[0] + 1
            wait()
            if not first:
                dve.wait_ge(xT_full, KT * k)
            for t in range(BLK):
                ins = nc.vector.tensor_scalar(xn[:, t, :], x_ln[:, t, :], mv[:, t, 0:1], rs[:, 3, t:t + 1],
                                              ALU.subtract, ALU.mult)
            ins.then_inc(xn_ready, 1)

        def rope(k, t):
            dve.wait_ge(pair_full, PAIRS * k + t + 1)
            if t >= 2 or not (isinstance(k, int) and k == 0):
                dve.wait_ge(qk_ready, BLK * k + t - 1)
            G = 2 * H
            a, b = 2 + 2 * (t % 2), 3 + 2 * (t % 2)
            qk = bank(a).rearrange("p (g s f) -> p g s f", g=G, s=2)
            rc = rot_c[:, t % 2, :].rearrange("p (g s f) -> p g s f", g=G, s=2)
            rsn = rot_s[:, t % 2, :].rearrange("p (g s f) -> p g s f", g=G, s=2)
            tile = k * BLK + t
            HF = DH // 2
            cos = cos_t[:, bass.ds(tile, 1), :].rearrange("p a f -> p (a f)")
            sin = sin_t[:, bass.ds(tile, 1), :].rearrange("p a f -> p (a f)")
            for s in range(2):
                nc.vector.tensor_tensor(rc[:, :, s, :], qk[:, :, s, :], cos.unsqueeze(1).to_broadcast([P, G, HF]), ALU.mult)
            for s in range(2):
                ins = nc.vector.tensor_tensor(rsn[:, :, s, :], qk[:, :, 1 - s, :],
                                              sin[:, s * HF:(s + 1) * HF].unsqueeze(1).to_broadcast([P, G, HF]), ALU.mult)
            ins.then_inc(rope_ready, 1)
            nc.vector.tensor_scalar(v_all[:, bass.ds(tile, 1), :, :].rearrange("p a h d -> p (a h d)"), bank(b, D), 1.0, None,
                                    ALU.mult).then_inc(pair_used, 1)

        def split(k, t):
            u = t % 2
            n = 3 * (BLK * k + t)
            dve.wait_ge(qk_ready, BLK * k + t + 1)
            if t >= 2 or not (isinstance(k, int) and k == 0):
                dve.wait_ge(partsT_full, BLK * k + t - 1)
            nc.vector.tensor_copy(parts[:, u, 0, :], qk_rot[:, u, :]).then_inc(split_step, 1)
            dve.wait_ge(split_step, n + 1)
            nc.vector.tensor_tensor(qk_rem[:, u, :], qk_rot[:, u, :], parts[:, u, 0, :], ALU.subtract).then_inc(split_step, 1)
            dve.wait_ge(split_step, n + 2)
            nc.vector.tensor_copy(parts[:, u, 1, :], qk_rem[:, u, :]).then_inc(split_step, 1)
            dve.wait_ge(split_step, n + 3)
            nc.vector.tensor_tensor(parts[:, u, 2, :], qk_rem[:, u, :], parts[:, u, 1, :], ALU.subtract).then_inc(parts_ready, 1)

        def gate_up(k, j):
            dve.wait_ge(silu_ready, HT * k + j + 1)
            dve.wait_ge(pair_full, PAIRS * k + BLK + j + 1)
            nc.vector.tensor_tensor(hT[:, j, :], bank(3 + 2 * (j % 2)), silu[:, j % 2, :], ALU.mult).then_inc(pair_used, 1)

        def add_x(k, t):
            dve.wait_ge(down_full, BLK * k + t + 1)
            if t == 0:
                dve.wait_ge(xres_loaded, 16 * (k + 1))
                if not (isinstance(k, int) and k == 0):
                    dve.wait_ge(y_out, 16 * k)
            nc.vector.tensor_tensor(y_blk[:, t, :], bank(6 + t % 2, D), x_res[:, t, :], ALU.add).then_inc(y_ready, 1)

        def block_a(k, last):
            rope(k, 0)
            rope(k, 1)
            split(k, 0)
            rope(k, 2)
            split(k, 1)
            rope(k, 3)
            split(k, 2)
            gate_up(k, 0)
            split(k, 3)
            for j in range(1, HT - 1):
                gate_up(k, j)
            if not last:
                row_stats(k + 1)
            gate_up(k, HT - 1)
            if not last:
                layer_norm(k + 1, False)
            for t in range(BLK):
                add_x(k, t)

        row_stats(0)
        layer_norm(0, True)
        dve.wait_ge(tables_loaded, 32)
        dve.wait_ge(wt_saved, WG)
        block_a(0, False)
        with dve.Fori(1, NBLK - 1) as k:
            block_a(k, False)
        block_a(NBLK - 1, True)

        dve.wait_ge(b_const, 4)

        def step(c, i):
            hl, t = divmod(c, TILES)
            h = head_of(c, TILES)
            if h is not None:
                n = 5 * (h + SLOTS * i)
                dve.wait_ge(s1_used, 2 * TILES * (h + 1 + SLOTS * i))
                nc.vector.tensor_reduce(neg_max[:, :], row_max[:, h % 2, :, :], AX.X, ALU.max, negate=True).then_inc(stab_step, 1)
                dve.wait_ge(stab_step, n + 1)
                nc.vector.tensor_copy(stab[:, 0, :], neg_max[:, :]).then_inc(stab_step, 1)
                dve.wait_ge(stab_step, n + 2)
                nc.vector.tensor_tensor(neg_rem[:, :], neg_max[:, :], stab[:, 0, :], ALU.subtract).then_inc(stab_step, 1)
                dve.wait_ge(stab_step, n + 3)
                nc.vector.tensor_copy(stab[:, 1, :], neg_rem[:, :]).then_inc(stab_step, 1)
                dve.wait_ge(stab_step, n + 4)
                nc.vector.tensor_tensor(stab[:, 2, :], neg_rem[:, :], stab[:, 1, :], ALU.subtract).then_inc(stab_step, 1)
            h = head_of(c, VCOPY_AT)
            if h is not None:
                if h >= 2:
                    dve.wait_ge(pv_done, TILES * (h - 1 + SLOTS * i))
                hh = h + SLOTS * i
                src = v_all[:, bass.ds(sequence_of(hh) * TILES, TILES), bass.ds(hh & (H - 1), 1), :].rearrange("p t a d -> p t (a d)")
                nc.vector.tensor_scalar(v_op[:, h % 2, :, 0:DH], src, 1.0, None, ALU.mult).then_inc(v_ready, 1)
            h = head_of(c, NORM_AT)
            if h is not None:
                g = TILES * h + TURN_AT
                dve.wait_ge(s2_used, items_before(g) + 1 + HEAD_ITEMS * SLOTS * i)
                turned = oT_sb[:, :].rearrange("p (n j d) -> p j n d", n=4, j=4)
                if h >= 1:
                    dve.wait_ge(o_ready, h + SLOTS * i)
                nc.vector.reciprocal(inv_sum[:, :, :], turned[:, :, :, DH]).then_inc(sum_inv, 1)
                dve.wait_ge(sum_inv, h + 1 + SLOTS * i)
                hh = h + SLOTS * i
                dst = o_all[:, bass.ds(sequence_of(hh) * TILES, TILES), bass.ds(hh & (H - 1), 1), :].rearrange(
                    "p (j n) a d -> p j n (a d)", j=4)
                nc.vector.tensor_tensor(dst, turned[:, :, :, 0:DH], inv_sum[:, :, :].unsqueeze(3).to_broadcast([P, 4, 4, DH]),
                                        ALU.mult).then_inc(o_ready, 1)
            if c < N1:
                for half in range(2):
                    dve.wait_ge(s1_full, 2 * c + half + 1 + 2 * UNROLL * i)
                    nc.vector.tensor_reduce(row_max[:, hl % 2, t, half:half + 1], psum[:, 2 * half * BANK:(2 * half + 2) * BANK],
                                            AX.X, ALU.max).then_inc(s1_used, 1)

        run_steps(dve, step)

        dve.wait_ge(o_ready, HEADS)

        def gather(n, j, first):
            k = 2 * n + j
            if not first:
                dve.wait_ge(cT_full, KT * (k - 1))
            nc.vector.tensor_scalar(o_blk[:, j, :, :], o_all[:, bass.ds(k * BLK, BLK), :, :].rearrange("p t h d -> p t (h d)"),
                                    1.0, None, ALU.mult).then_inc(c_gathered, 1)

        def add_y(n, j, first):
            k = 2 * n + j
            dve.wait_ge(yin_loaded[j], 16 * (n + 1))
            if not first:
                dve.wait_ge(res_out[j], 16 * n)
            for u in range(2):
                dve.wait_ge(proj_full, 2 * k + u + 1)
                nc.vector.tensor_tensor(res[:, j, 2 * u:2 * u + 2, :], bank(4 + 2 * j + u).rearrange("p (t d) -> p t d", t=2),
                                        y_in[:, j, 2 * u:2 * u + 2, :], ALU.add).then_inc(res_ready, 1)

        for j in range(2):
            gather(0, j, True)
        for j in range(2):
            add_y(0, j, True)
        with dve.Fori(1, NBLK // 2) as n:
            for j in range(2):
                gather(n, j, False)
            for j in range(2):
                add_y(n, j, False)

    keep.close()


def kernel(**inputs):
    import numpy as np
    import concourse.bacc as bacc
    from concourse.bass_utils import run_bass_kernel_spmd

    xs = np.ascontiguousarray(inputs["L0_attn_x"])
    nb, L, D = xs.shape
    n_tok = nb * L
    half = DH // 2
    inv_freq = (np.float32(1.0) / np.power(np.float32(10000.0), np.arange(half, dtype=np.float32) / np.float32(half))).astype(np.float32)
    ang = np.arange(L, dtype=np.float32)[:, None] * inv_freq[None, :]
    cos, sin = np.cos(ang).astype(np.float32), np.sin(ang).astype(np.float32)
    cos = np.tile(cos, (nb, 1)).reshape(n_tok // P, P, half).transpose(1, 0, 2)
    sin = np.tile(np.concatenate([-sin, sin], axis=1), (nb, 1)).reshape(n_tok // P, P, DH).transpose(1, 0, 2)

    arrays = {
        "in_x": xs.reshape(n_tok, D),
        "in_w_qkv": np.ascontiguousarray(inputs["L0_attn_w_qkv"]),
        "in_w_out": np.ascontiguousarray(inputs["L0_attn_w_out"]),
        "in_w_gate": np.ascontiguousarray(inputs["L0_ffn_w_gate"]),
        "in_w_up": np.ascontiguousarray(inputs["L0_ffn_w_up"]),
        "in_w_down": np.ascontiguousarray(inputs["L0_ffn_w_down"]),
        "in_cos": np.ascontiguousarray(cos),
        "in_sin": np.ascontiguousarray(sin),
        "in_ident": np.eye(P, dtype=np.float32),
    }
    nc = bacc.Bacc("TRN2", target_bir_lowering=False, num_devices=1)
    ins = [nc.dram_tensor(n, a.shape, mybir.dt.from_np(a.dtype), kind="ExternalInput").ap() for n, a in arrays.items()]
    out = nc.dram_tensor("out_y", (n_tok, D), F32, kind="ExternalOutput").ap()
    y_dram = nc.dram_tensor("y_dram", (n_tok, D), F32, kind="Internal").ap()
    qk_dram = nc.dram_tensor("qk_dram", (2, PARTS, D, n_tok), BF16, kind="Internal").ap()
    layer_program(nc, *ins, out, y_dram, qk_dram)
    r = run_bass_kernel_spmd(nc, [arrays], core_ids=[0])
    return r.results[0]["out_y"].reshape(nb, L, D)
```

```python
from contextlib import ExitStack

import concourse.bass as bass
from concourse import mybir

F32 = mybir.dt.float32
BF16 = mybir.dt.bfloat16
F16 = mybir.dt.float16
I32 = mybir.dt.int32
ALU = mybir.AluOpType
ACT = mybir.ActivationFunctionType
AX = mybir.AxisListType
RMAX = bass.bass_isa.ReduceOp.max

P = 128
DH = 16
BANK = 512
TILES = 16
BLK = 4
PARTS = 3
Q_PART = [0, 1, 2, 0, 1, 0]
K_PART = [0, 0, 0, 1, 1, 2]
ROWS = len(Q_PART) * DH
SLOTS = 4
LAG = 3
RING = 3
UNROLL = SLOTS * TILES
PRODUCTS = [(0, 0), (0, 1), (1, 0)]
EPS = 1e-5
QUANT_SCALE = 1.0 / 127.0
X_SCALE = 2.0 ** 11
W_SCALE = 2.0 ** 13
H_SCALE = 2.0 ** 10
EXPONENT = 0x7F800000
TWO_EXPONENTS = float(254 << 23)


def layer_program(nc, x, w_qkv, w_out, w_gate, w_up, w_down, cos_tab, sin_tab, ident_in, out, y_dram, qk_dram):
    TOKENS, D = x.shape
    HID = w_gate.shape[0]
    H = D // DH
    KT = D // P
    HT = HID // P
    NT = TOKENS // P
    NBLK = NT // BLK
    HEADS = (TOKENS // (TILES * P)) * H
    SCALE = float(DH) ** -0.5
    assert D == 256 and KT == 2 and HEADS % SLOTS == 0

    x_blocks = x.rearrange("(k t p) d -> k p t d", p=P, t=BLK)
    y_blocks = y_dram.rearrange("(k t p) d -> k p t d", p=P, t=BLK)
    out_blocks = out.rearrange("(k t p) d -> k p t d", p=P, t=BLK)

    keep = ExitStack()

    def sb(stack, name, shape, dt=F32):
        return stack.enter_context(nc.sbuf_tensor(name, shape, dt))

    def sem(name):
        return keep.enter_context(nc.semaphore(name))

    ident = sb(keep, "ident", [P, P])
    ident16 = sb(keep, "ident16", [P, P], BF16)
    identh = sb(keep, "identh", [P, P], F16)
    v_space = sb(keep, "v_space", [P, max(NT * D, (3 * D * D + 3 * 2 * HID * D + D * D + (3 * D + 2 * HID) * D) // P)])
    v_all = v_space[:, 0:NT * D].rearrange("p (t h d) -> p t h d", h=H, d=DH)
    woT = sb(keep, "woT", [P, KT, D])
    sa = ExitStack()
    WCOLS = 3 * KT * D + 2 * KT * HID
    w16 = sb(sa, "w16", [P, 2, WCOLS], F16)
    o0 = 0
    wqkvT = w16[:, :, o0:o0 + KT * 3 * D].rearrange("p a (k e) -> p a k e", k=KT)
    o0 += KT * 3 * D
    wgT = w16[:, :, o0:o0 + KT * HID].rearrange("p a (k e) -> p a k e", k=KT)
    o0 += KT * HID
    wuT = w16[:, :, o0:o0 + KT * HID].rearrange("p a (k e) -> p a k e", k=KT)
    wdT = sb(sa, "wdT", [P, 2, HT, D], F16)
    NROW = 3 * D // P + 2 * HT
    largest = sb(sa, "largest", [P, NROW])
    row_max1 = sb(sa, "row_max1", [P, 2 * HT])
    pow_gu = sb(sa, "pow_gu", [P, 2 * HT])
    inv_gu = sb(sa, "inv_gu", [P, 2 * HT])
    scale_gu = sb(sa, "scale_gu", [P, 2 * HT])
    gate_fix = sb(sa, "gate_fix", [P, HT])
    h_fix = sb(sa, "h_fix", [P, HT])
    pow_prod = sb(sa, "pow_prod", [P, HT])
    h_inv = sb(sa, "h_inv", [P, HT])
    mat_max = sb(sa, "mat_max", [P, 3, 2])
    down_max = sb(sa, "down_max", [P, 3, 1])
    pow_m = sb(sa, "pow_m", [P, 3])
    inv_m = sb(sa, "inv_m", [P, 3])
    scale_m = sb(sa, "scale_m", [P, 3])
    fix_m = sb(sa, "fix_m", [P, 3])
    cos_t = sb(sa, "cos_t", [P, NT, DH // 2])
    sin_t = sb(sa, "sin_t", [P, NT, DH])
    x_ln = sb(sa, "x_ln", [P, BLK, D])
    x_res = sb(sa, "x_res", [P, BLK, D])
    stats = sb(sa, "stats", [P, BLK, 6])
    mv = sb(sa, "mv", [P, BLK, 2])
    ve = sb(sa, "ve", [P, BLK])
    seed = sb(sa, "seed", [P, BLK], I32)
    rs = sb(sa, "rs", [P, 4, BLK])
    nt_a = sb(sa, "nt_a", [P, 3, BLK])
    nt_b = sb(sa, "nt_b", [P, 3, BLK])
    xn = sb(sa, "xn", [P, BLK, D])
    xnT = sb(sa, "xnT", [P, 2, KT, BLK * P], F16)
    rot_c = sb(sa, "rot_c", [P, 2, 2 * D])
    rot_s = sb(sa, "rot_s", [P, 2, 2 * D])
    qk_rot = sb(sa, "qk_rot", [P, 2, 2 * D])
    qk_rem = sb(sa, "qk_rem", [P, 2, 2 * D])
    parts = sb(sa, "parts", [P, 2, PARTS, 2 * D], BF16)
    staged = sb(sa, "staged", [P, PARTS, 2 * KT, BLK * P], BF16)
    silu = sb(sa, "silu", [P, 2, BANK])
    h32 = sb(sa, "h32", [P, 2, BANK])
    hT = sb(sa, "hT", [P, 2, HT, BLK * P], F16)
    y_blk = sb(sa, "y_blk", [P, BLK, D])
    n0 = 0
    nat = {}
    for nm, rows, cols in (("qkv", 3 * D, D), ("g", HID, D), ("u", HID, D), ("o", D, D), ("d", D, HID),
                           ("gi", HID, D), ("ui", HID, D), ("di", D, HID)):
        n = rows // P * cols
        nat[nm] = v_space[:, n0:n0 + n]
        if nm.endswith("i"):
            nat[nm] = nat[nm].bitcast(I32)
        nat[nm] = nat[nm].rearrange("p (t c) -> p t c", c=cols)
        n0 += n
    n16 = NROW * D // 2
    nat16 = v_space[:, n0:n0 + 2 * n16].bitcast(F16).rearrange("p (a t c) -> p a t c", a=2, c=D)
    n0 += 2 * n16
    wdT32 = nat["gi"].rearrange("p t c -> p (t c)").bitcast(F32).rearrange("p (t c) -> p t c", c=D)
    sa.close()

    sB = ExitStack()
    o_all = sb(sB, "o_all", [P, NT, H, DH])
    q_op = sb(sB, "q_op", [P, SLOTS, TILES * P], BF16)
    k_op = sb(sB, "k_op", [P, SLOTS, TILES * P], BF16)
    probs = sb(sB, "probs", [P, 2, TILES * P])
    v_op = sb(sB, "v_op", [P, 2, TILES, 32])
    row_max = sb(sB, "row_max", [P, 2, TILES, 2])
    neg_max = sb(sB, "neg_max", [P, TILES])
    neg_rem = sb(sB, "neg_rem", [P, TILES])
    zero = sb(sB, "zero", [P, TILES])
    stab = sb(sB, "stab", [P, P // TILES, TILES], BF16)
    stabT = sb(sB, "stabT", [PARTS * TILES, P], BF16)
    acc_sb = sb(sB, "acc_sb", [P, BANK])
    oT_sb = sb(sB, "oT_sb", [P, BANK])
    inv_sum = sb(sB, "inv_sum", [P, 4, 4])
    sB.close()
    n_c = BLK * D
    o_blk, oT, y_in, res = (v_space[:, 2 * n * n_c:2 * (n + 1) * n_c] for n in range(4))
    o_blk, y_in, res = (a.rearrange("p (j t d) -> p j t d", j=2, t=BLK) for a in (o_blk, y_in, res))
    oT = oT.rearrange("p (j k n) -> p j k n", j=2, k=KT)

    psum = keep.enter_context(nc.psum_tensor("psum", [P, 8 * BANK], F32))

    def bank(n, cols=BANK):
        return psum[:, n * BANK:n * BANK + cols]

    w_loaded = sem("w_loaded")
    ident_loaded = sem("ident_loaded")
    tables_loaded = sem("tables_loaded")
    ident16_ready = sem("ident16_ready")
    prep = sem("prep")
    mat_reduced = sem("mat_reduced")
    hi_ready = sem("hi_ready")
    lo_ready = sem("lo_ready")
    down_ready = sem("down_ready")
    wd_full = sem("wd_full")
    wd_saved = sem("wd_saved")
    wt_full = sem("wt_full")
    wt_saved = sem("wt_saved")
    x_loaded = sem("x_loaded")
    xres_loaded = sem("xres_loaded")
    ln_step = sem("ln_step")
    xn_ready = sem("xn_ready")
    xT_full = sem("xT_full")
    xT_saved = sem("xT_saved")
    xlo_ready = sem("xlo_ready")
    pair_full = sem("pair_full")
    pair_used = sem("pair_used")
    silu_ready = sem("silu_ready")
    hhi_ready = sem("hhi_ready")
    hlo_ready = sem("hlo_ready")
    rope_ready = sem("rope_ready")
    qk_ready = sem("qk_ready")
    part_hi = sem("part_hi")
    rem_ready = sem("rem_ready")
    part_mid = sem("part_mid")
    parts_ready = sem("parts_ready")
    partsT_full = sem("partsT_full")
    partsT_saved = sem("partsT_saved")
    staged_out = sem("staged_out")
    down_full = sem("down_full")
    y_ready = sem("y_ready")
    y_out = sem("y_out")
    b_const = sem("b_const")
    qk_loaded = [sem(f"qk_loaded{s}") for s in range(SLOTS)]
    stab_loaded = sem("stab_loaded")
    s1_full = sem("s1_full")
    s1_used = sem("s1_used")
    s2_full = sem("s2_full")
    s2_used = sem("s2_used")
    pv_done = sem("pv_done")
    acc_saved = sem("acc_saved")
    v_ready = sem("v_ready")
    max_ready = sem("max_ready")
    stab_step = sem("stab_step")
    sum_inv = sem("sum_inv")
    o_ready = sem("o_ready")
    c_gathered = sem("c_gathered")
    cT_full = sem("cT_full")
    cT_saved = sem("cT_saved")
    proj_full = sem("proj_full")
    yin_loaded = [sem("yin_loaded0"), sem("yin_loaded1")]
    res_ready = sem("res_ready")
    res_out = [sem("res_out0"), sem("res_out1")]

    wt_blocks = [(a, r0 + j, k) for a in range(2) for r0, n in ((0, 3 * D // P), (3 * D // P, HT), (3 * D // P + HT, HT))
                 for k in range(KT) for j in range(n)]
    WG = len(wt_blocks) // 8

    PAIRS = BLK + HT
    PAIR_BANK = [2, 4, 6, 2, 4, 2, 4, 2, 4, 2]
    DOWN_BANK = [6, 7, 4, 5]
    LN_STEPS = 5 + 3 * 4
    N_STAGED = 2 * KT

    N1 = HEADS * TILES
    FIRST2 = TILES + LAG
    STAB_AT = TILES + 1
    SAVE_AT = FIRST2 + TILES + 1
    TURN_AT = SAVE_AT + 1
    NORM_AT = TURN_AT + 1
    VCOPY_AT = 10
    STEPS_B = N1 + (NORM_AT - TILES) + 1
    HEAD_ITEMS = 4 * TILES + 2
    assert HEAD_ITEMS % RING == 0
    PRO = NORM_AT
    BODIES = (N1 - PRO) // UNROLL

    def head_of(g, at):
        h, r = divmod(g - at, TILES)
        return h if r == 0 and 0 <= h < HEADS else None

    def sequence_of(h):
        n = h >> (H.bit_length() - 1)
        if not isinstance(h, int):
            n.max_val = HEADS // H - 1
        return n

    def before(g, at):
        return min(max((g - at + TILES - 1) // TILES, 0), HEADS)

    def items_before(g):
        return 4 * min(max(g - FIRST2, 0), N1) + before(g, STAB_AT) + before(g, TURN_AT)

    def extra_items(g):
        return (head_of(g, STAB_AT) is not None) + (head_of(g, TURN_AT) is not None)

    def run_steps(eng, step):
        for c in range(PRO):
            step(c, 0)
        if BODIES:
            with eng.Fori(0, BODIES) as i:
                for c in range(PRO, PRO + UNROLL):
                    step(c, i)
        for c in range(PRO + UNROLL * BODIES, STEPS_B):
            step(c, 0)

    MAT_MAX_READY, SCALES_READY, DOWN_SPLIT = 8, 21, 30

    def nat_row(r):
        nq = 3 * D // P
        if r < nq:
            m = 1 if r >= 2 * D // P else 0
            return nat["qkv"][:, r, :], scale_m[:, m:m + 1]
        n = r - nq
        return nat["g" if n < HT else "u"][:, n % HT, :], scale_gu[:, n:n + 1]

    block = keep.enter_context(nc.Block())

    @block.sync
    def _(sp):
        sp.dma_start(ident[:, :], ident_in).then_inc(ident_loaded, 16)
        sp.dma_start(nat["qkv"], w_qkv.rearrange("(t p) c -> p t c", p=P)).then_inc(w_loaded, 16)
        sp.dma_start(nat["o"], w_out.rearrange("(t p) c -> p t c", p=P)).then_inc(w_loaded, 16)
        sp.dma_start(nat["gi"], w_gate.rearrange("(t p) c -> p t c", p=P)).then_inc(w_loaded, 16)
        sp.dma_start(nat["ui"], w_up.rearrange("(t p) c -> p t c", p=P)).then_inc(w_loaded, 16)
        sp.dma_start(nat["di"], w_down.rearrange("(t p) c -> p t c", p=P)).then_inc(w_loaded, 16)
        sp.dma_start(x_ln[:, :, :], x_blocks[0]).then_inc(x_loaded, 16)
        sp.dma_start(cos_t[:, :, :], cos_tab).then_inc(tables_loaded, 16)
        sp.dma_start(sin_t[:, :, :], sin_tab).then_inc(tables_loaded, 16)

        def block_a(k, last):
            if not (isinstance(k, int) and k == 0):
                sp.wait_ge(y_ready, BLK * k)
            sp.dma_start(x_res[:, :, :], x_blocks[k]).then_inc(xres_loaded, 16)
            if not last:
                sp.wait_ge(xn_ready, k + 1)
                sp.dma_start(x_ln[:, :, :], x_blocks[k + 1]).then_inc(x_loaded, 16)
            sp.wait_ge(partsT_saved, BLK * (k + 1))
            for qg in range(2 * KT):
                dst = qk_dram[qg // KT, :, (qg % KT) * P:(qg % KT + 1) * P, bass.ds(k * (BLK * P), BLK * P)]
                sp.dma_start(dst.rearrange("a r n -> r a n"), staged[:, :, qg, :]).then_inc(staged_out, 16)
            sp.wait_ge(y_ready, BLK * (k + 1))
            sp.dma_start(y_blocks[k], y_blk[:, :, :]).then_inc(y_out, 16)

        block_a(0, False)
        with sp.Fori(1, NBLK - 1) as k:
            block_a(k, False)
        block_a(NBLK - 1, True)

        sp.wait_ge(staged_out, 16 * N_STAGED * NBLK)
        sp.wait_ge(y_out, 16 * NBLK)
        sp.wait_ge(down_full, BLK * NBLK)

        def load_head(hl, i):
            h = hl + SLOTS * i
            s = hl % SLOTS
            head = (h & (H - 1)) * DH
            tok = sequence_of(h) * (TILES * P)
            src = qk_dram[:, :, bass.ds(head, DH), bass.ds(tok, TILES * P)]
            r = 0
            for n in (3, 2, 1):
                sp.dma_start(q_op[r * DH:(r + n) * DH, s, :], src[0, 0:n]).then_inc(qk_loaded[s], 16)
                r += n
            for r in range(len(K_PART)):
                sp.dma_start(k_op[r * DH:(r + 1) * DH, s, :], src[1, K_PART[r]]).then_inc(qk_loaded[s], 16)

        def load_stab(hl, i):
            h = hl + SLOTS * i
            g = TILES * hl + STAB_AT
            sp.wait_ge(s2_used, items_before(g) + 1 + HEAD_ITEMS * SLOTS * i)
            dst = q_op[ROWS:ROWS + PARTS, hl % SLOTS, :].rearrange("a (t n) -> a t n", t=TILES)
            sp.dma_start(dst, stabT[:, :]).then_inc(stab_loaded, 16)

        load_head(0, 0)
        load_head(1, 0)
        for hl in range(SLOTS):
            load_stab(hl, 0)
            load_head(hl + 2, 0)
        with sp.Fori(0, HEADS // SLOTS - 2) as i:
            for hl in range(SLOTS, 2 * SLOTS):
                load_stab(hl, i)
                load_head(hl + 2, i)
        for hl in range(HEADS - SLOTS, HEADS):
            load_stab(hl, 0)
            if hl + 2 < HEADS:
                load_head(hl + 2, 0)

        sp.wait_ge(o_ready, HEADS)

        def load_y(n, j):
            sp.dma_start(y_in[:, j], y_blocks[2 * n + j]).then_inc(yin_loaded[j], 16)

        def store_out(n, j):
            sp.wait_ge(res_ready, 2 * (2 * n + j + 1))
            sp.dma_start(out_blocks[2 * n + j], res[:, j]).then_inc(res_out[j], 16)

        for j in range(2):
            load_y(0, j)
        with sp.Fori(0, NBLK // 2 - 1) as n:
            for j in range(2):
                store_out(n, j)
                load_y(n + 1, j)
        for j in range(2):
            store_out(NBLK // 2 - 1, j)
        for j in range(2):
            sp.wait_ge(res_out[j], 16 * (NBLK // 2))

    @block.tensor
    def _(pe):
        pe.wait_ge(ident_loaded, 16)
        pe.wait_ge(w_loaded, 80)
        pe.wait_ge(prep, 3)
        for k in range(KT):
            for j in range(D // P):
                n = k * (D // P) + j
                mm = pe.transpose(bank(0)[:, n * P:(n + 1) * P], nat["o"][:, j, k * P:(k + 1) * P], ident[:, :])
        mm.then_inc(wd_full, 1)
        for k in range(HT):
            for j in range(D // P):
                n = k * (D // P) + j
                mm = pe.transpose(psum[:, BANK + n * P:BANK + (n + 1) * P], nat["d"][:, j, k * P:(k + 1) * P], ident[:, :])
        mm.then_inc(wd_full, 1)
        pe.wait_ge(ident16_ready, 2)
        pe.wait_ge(hi_ready, NROW)
        pe.wait_ge(lo_ready, NROW)
        for grp in range(WG):
            if grp >= 4:
                pe.wait_ge(wt_saved, grp - 3)
            for j in range(8):
                a, r, c = wt_blocks[8 * grp + j]
                mm = pe.transpose(bank(4 + grp % 4).bitcast(F16)[:, j * P:(j + 1) * P], nat16[:, a, r, c * P:(c + 1) * P],
                                  identh[:, :])
            mm.then_inc(wt_full, 1)
        pe.wait_ge(wt_saved, WG)
        pe.wait_ge(wd_saved, 1 + HT)

        def turn_x(k, first):
            pe.wait_ge(xn_ready, k + 1)
            if not first:
                pe.wait_ge(partsT_saved, BLK * k)
            for c in range(KT):
                for t in range(BLK):
                    mm = pe.transpose(bank(c)[:, t * P:(t + 1) * P], xn[:, t, c * P:(c + 1) * P], ident[:, :])
                mm.then_inc(xT_full, 1)

        def block_a(k, last):
            def take_pair(u):
                if u in (1, 2):
                    if not (isinstance(k, int) and k == 0):
                        pe.wait_ge(y_ready, BLK * k)
                elif u == 0:
                    if not (isinstance(k, int) and k == 0):
                        pe.wait_ge(pair_used, PAIRS * k)
                else:
                    before_u = max(v for v in range(u) if PAIR_BANK[v] == PAIR_BANK[u])
                    pe.wait_ge(pair_used, PAIRS * k + before_u + 1)
                return PAIR_BANK[u]

            for t in range(BLK):
                if t == 0:
                    pe.wait_ge(xT_saved, KT * (k + 1))
                    pe.wait_ge(xlo_ready, KT * (k + 1))
                a = take_pair(t)
                for dst, e0, e1 in ((bank(a), 0, 2 * D), (bank(a + 1, D), 2 * D, 3 * D)):
                    for c in range(KT):
                        for n, (xp, wp) in enumerate(PRODUCTS):
                            mm = pe.matmul(dst, xnT[:, xp, c, t * P:(t + 1) * P], wqkvT[:, wp, c, e0:e1],
                                           start=(c == 0 and n == 0), stop=(c == KT - 1 and n == 2))
                mm.then_inc(pair_full, 1)
            for j in range(HT):
                a = take_pair(BLK + j)
                for w, dst in ((wgT, a), (wuT, a + 1)):
                    for c in range(KT):
                        for n, (xp, wp) in enumerate(PRODUCTS):
                            mm = pe.matmul(bank(dst), w[:, wp, c, j * P:(j + 1) * P], xnT[:, xp, c, :],
                                           start=(c == 0 and n == 0), stop=(c == KT - 1 and n == 2))
                mm.then_inc(pair_full, 1)
                if 1 <= j <= BLK:
                    t = j - 1
                    pe.wait_ge(parts_ready, BLK * k + t + 1)
                    if t == 0:
                        pe.wait_ge(xT_saved, KT * (k + 1))
                        pe.wait_ge(xlo_ready, KT * (k + 1))
                    else:
                        pe.wait_ge(partsT_saved, BLK * k + t)
                    turned = psum[:, 0:2 * BANK].bitcast(BF16)
                    for n in range(PARTS * 2 * KT):
                        a, qg = divmod(n, 2 * KT)
                        mm = pe.transpose(turned[:, n * P:(n + 1) * P], parts[:, t % 2, a, qg * P:(qg + 1) * P], ident16[:, :])
                    mm.then_inc(partsT_full, 1)
            if not last:
                turn_x(k + 1, False)

            def down(t, hidden):
                for j in hidden:
                    for n, (hp, wp) in enumerate(PRODUCTS):
                        mm = pe.matmul(bank(DOWN_BANK[t], D), hT[:, hp, j, t * P:(t + 1) * P], wdT[:, wp, j, :],
                                       start=(j == 0 and n == 0), stop=(j == HT - 1 and n == 2))
                return mm

            pe.wait_ge(hhi_ready, HT * (k + 1) - 1)
            pe.wait_ge(hlo_ready, HT * (k + 1) - 1)
            for t in range(2):
                down(t, range(HT - 1))
            pe.wait_ge(hhi_ready, HT * (k + 1))
            pe.wait_ge(hlo_ready, HT * (k + 1))
            for t in range(2):
                down(t, [HT - 1]).then_inc(down_full, 1)
            for t in range(2, BLK):
                if t == 2:
                    pe.wait_ge(pair_used, PAIRS * (k + 1) - 1)
                down(t, range(HT)).then_inc(down_full, 1)

        pe.wait_ge(prep, DOWN_SPLIT)
        turn_x(0, True)
        block_a(0, False)
        with pe.Fori(1, NBLK - 1) as k:
            block_a(k, False)
        block_a(NBLK - 1, True)

        pe.wait_ge(b_const, 5)
        pe.wait_ge(y_ready, BLK * NBLK)
        pe.wait_ge(partsT_saved, BLK * NBLK)

        def max_half(c, i, half):
            hl, t = divmod(c, TILES)
            if t == 0 and half == 0:
                nd = 16 * (3 + len(K_PART))
                pe.wait_ge(qk_loaded[hl % SLOTS], nd * (hl // SLOTS + 1 + i))
            n = 2 * c + half
            if n >= 2:
                pe.wait_ge(s1_used, n - 1 + 2 * UNROLL * i)
            s = hl % SLOTS
            for j in range(2):
                cols = (2 * half + j) * BANK
                mm = pe.matmul(bank(2 * half + j), q_op[0:ROWS, s, t * P:(t + 1) * P], k_op[0:ROWS, s, cols:cols + BANK],
                               start=True, stop=True)
            mm.then_inc(s1_full, 1)

        def step(c, i):
            item = items_before(c)

            def take_bank(item):
                if item >= RING:
                    pe.wait_ge(s2_used, item - RING + 1 + HEAD_ITEMS * SLOTS * i)
                return 4 + item % RING

            if c < N1:
                max_half(c, i, 0)
            h = head_of(c, STAB_AT)
            if h is not None:
                pe.wait_ge(stab_step, 4 * (h + 1 + SLOTS * i))
                b = take_bank(item)
                pe.transpose(bank(b).bitcast(BF16)[:, 0:P], stab[:, :, :].rearrange("p a t -> p (a t)"),
                             ident16[:, :]).then_inc(s2_full, 1)
                item += 1
            h = head_of(c, TURN_AT)
            if h is not None:
                pe.wait_ge(acc_saved, h + 1 + SLOTS * i)
                b = take_bank(item)
                for n in range(4):
                    mm = pe.transpose(bank(b)[:, n * P:(n + 1) * P], acc_sb[:, n * P:(n + 1) * P], ident[:, :])
                mm.then_inc(s2_full, 1)
                item += 1
            g2 = c - FIRST2
            for j in range(4):
                if j == 2 and c < N1:
                    max_half(c, i, 1)
                if 0 <= g2 < N1:
                    h, t = divmod(g2, TILES)
                    if t == 0 and j == 0:
                        pe.wait_ge(stab_loaded, 16 * (h + 1 + SLOTS * i))
                    b = take_bank(item)
                    pe.matmul(bank(b), k_op[0:ROWS + PARTS, h % SLOTS, t * P:(t + 1) * P],
                              q_op[0:ROWS + PARTS, h % SLOTS, j * BANK:(j + 1) * BANK],
                              start=True, stop=True).then_inc(s2_full, 1)
                    item += 1
            g3 = g2 - 1
            if 0 <= g3 < N1:
                h, t = divmod(g3, TILES)
                if t == 0:
                    pe.wait_ge(v_ready, h + 1 + SLOTS * i)
                    if h >= 1:
                        pe.wait_ge(acc_saved, h + SLOTS * i)
                pe.wait_ge(s2_used, items_before(c - 1) + extra_items(c - 1) + 4 + HEAD_ITEMS * SLOTS * i)
                for j in range(4):
                    mm = pe.matmul(bank(7)[32 * j:32 * j + 32, :], v_op[:, h % 2, t, :], probs[:, g3 % 2, j * BANK:(j + 1) * BANK],
                                   start=(t == 0), stop=(t == TILES - 1), tile_position=(0, 32 * j))
                mm.then_inc(pv_done, 1)

        run_steps(pe, step)

        def block_c(n, j, first):
            k = 2 * n + j
            pe.wait_ge(c_gathered, k + 1)
            if not first:
                pe.wait_ge(cT_saved, KT * (k - 1))
            for c in range(KT):
                for t in range(BLK):
                    mm = pe.transpose(bank(2 * j + c)[:, t * P:(t + 1) * P], o_blk[:, j, t, c * P:(c + 1) * P], ident[:, :])
                mm.then_inc(cT_full, 1)

        def block_c2(n, j, first):
            k = 2 * n + j
            pe.wait_ge(cT_saved, KT * (k + 1))
            if not first:
                pe.wait_ge(res_ready, 2 * (k - 1))
            for t in range(BLK):
                for c in range(KT):
                    mm = pe.matmul(psum[:, (4 + 2 * j) * BANK + t * D:(4 + 2 * j) * BANK + (t + 1) * D],
                                   oT[:, j, c, t * P:(t + 1) * P], woT[:, c, :], start=(c == 0), stop=(c == KT - 1))
                if t % 2 == 1:
                    mm.then_inc(proj_full, 1)

        pe.wait_ge(s1_used, 2 * N1)
        pe.wait_ge(s2_used, items_before(STEPS_B))
        for j in range(2):
            block_c(0, j, True)
        for j in range(2):
            block_c2(0, j, True)
        with pe.Fori(1, NBLK // 2) as n:
            for j in range(2):
                block_c(n, j, False)
            for j in range(2):
                block_c2(n, j, False)

    @block.scalar
    def _(act):
        act.wait_ge(prep, SCALES_READY)
        for r in range(NROW):
            src, sc = nat_row(r)
            nc.scalar.activation(nat16[:, 0, r, :], src, ACT.Copy, scale=sc).then_inc(hi_ready, 1)
        act.wait_ge(wd_full, 1)
        nc.scalar.activation(woT[:, :, :].rearrange("p k e -> p (k e)"), bank(0), ACT.Copy).then_inc(wd_saved, 1)
        act.wait_ge(wd_full, 2)
        for j in range(HT):
            nc.scalar.activation(wdT32[:, j, :], psum[:, BANK + j * D:BANK + (j + 1) * D], ACT.Copy,
                                 scale=h_inv[:, j:j + 1]).then_inc(wd_saved, 1)
        w_flat = w16[:, :, :].rearrange("p a n -> p (a n)")
        for grp in range(WG):
            act.wait_ge(wt_full, grp + 1)
            nc.scalar.activation(w_flat[:, grp * 8 * P:(grp + 1) * 8 * P], bank(4 + grp % 4).bitcast(F16),
                                 ACT.Copy).then_inc(wt_saved, 1)

        def h_hi(k, j):
            act.wait_ge(pair_used, PAIRS * k + BLK + j + 1)
            nc.scalar.activation(hT[:, 0, j, :], h32[:, j % 2, :], ACT.Copy).then_inc(hhi_ready, 1)

        def x_hi(k):
            for c in range(KT):
                act.wait_ge(xT_full, KT * k + c + 1)
                nc.scalar.activation(xnT[:, 0, c, :], bank(c), ACT.Copy, scale=X_SCALE).then_inc(xT_saved, 1)

        def hi_part(k, t):
            act.wait_ge(qk_ready, BLK * k + t + 1)
            if t >= 2 or not (isinstance(k, int) and k == 0):
                act.wait_ge(partsT_full, BLK * k + t - 1)
            nc.scalar.activation(parts[:, t % 2, 0, :], qk_rot[:, t % 2, :], ACT.Copy).then_inc(part_hi, 1)

        def block_a(k, last):
            hi_part(k, 0)
            hi_part(k, 1)
            for j in range(HT):
                act.wait_ge(pair_full, PAIRS * k + BLK + j + 1)
                nc.scalar.activation(silu[:, j % 2, :], bank(PAIR_BANK[BLK + j]), ACT.Silu,
                                     scale=gate_fix[:, j:j + 1]).then_inc(silu_ready, 1)
                if 1 <= j <= BLK:
                    t = j - 1
                    if t == 0 and not (isinstance(k, int) and k == 0):
                        act.wait_ge(staged_out, 16 * N_STAGED * k)
                    act.wait_ge(partsT_full, BLK * k + t + 1)
                    nc.scalar.activation(staged[:, :, :, t * P:(t + 1) * P],
                                         psum[:, 0:2 * BANK].bitcast(BF16)[:, 0:PARTS * 2 * KT * P].rearrange(
                                             "p (a q n) -> p a q n", a=PARTS, q=2 * KT),
                                         ACT.Copy).then_inc(partsT_saved, 1)
                    if t < 2:
                        hi_part(k, t + 2)
                h_hi(k, j)
            if not last:
                x_hi(k + 1)

        x_hi(0)
        block_a(0, False)
        with act.Fori(1, NBLK - 1) as k:
            block_a(k, False)
        block_a(NBLK - 1, True)

        act.wait_ge(down_full, BLK * NBLK)
        act.wait_ge(y_ready, BLK * NBLK)
        act.wait_ge(y_out, 16 * NBLK)
        act.wait_ge(staged_out, 16 * N_STAGED * NBLK)

        def step(c, i):
            item = items_before(c)

            def arrived(item):
                act.wait_ge(s2_full, item + 1 + HEAD_ITEMS * SLOTS * i)
                return 4 + item % RING

            h = head_of(c, SAVE_AT)
            if h is not None:
                act.wait_ge(pv_done, TILES * (h + 1 + SLOTS * i))
                nc.scalar.activation(acc_sb[:, :], bank(7), ACT.Copy).then_inc(acc_saved, 1)
            h = head_of(c, STAB_AT)
            if h is not None:
                if h >= 1:
                    act.wait_ge(stab_loaded, 16 * (h + SLOTS * i))
                b = arrived(item)
                nc.scalar.activation(stabT[:, :], bank(b).bitcast(BF16)[0:PARTS * TILES, 0:P], ACT.Copy).then_inc(s2_used, 1)
                item += 1
            h = head_of(c, TURN_AT)
            if h is not None:
                if h >= 1:
                    act.wait_ge(o_ready, h + SLOTS * i)
                b = arrived(item)
                nc.scalar.activation(oT_sb[:, :], bank(b), ACT.Copy).then_inc(s2_used, 1)
                item += 1
            g2 = c - FIRST2
            if 0 <= g2 < N1:
                if g2 >= 2:
                    act.wait_ge(pv_done, g2 - 1 + UNROLL * i)
                for j in range(4):
                    b = arrived(item)
                    nc.scalar.activation(probs[:, g2 % 2, j * BANK:(j + 1) * BANK], bank(b), ACT.Exp,
                                         scale=SCALE).then_inc(s2_used, 1)
                    item += 1

        run_steps(act, step)

        def block_c(n, j, first):
            k = 2 * n + j
            if not first:
                act.wait_ge(proj_full, 2 * (k - 1))
            for c in range(KT):
                act.wait_ge(cT_full, KT * k + c + 1)
                nc.scalar.activation(oT[:, j, c, :], bank(2 * j + c), ACT.Copy).then_inc(cT_saved, 1)

        for j in range(2):
            block_c(0, j, True)
        with act.Fori(1, NBLK // 2) as n:
            for j in range(2):
                block_c(n, j, False)

    @block.gpsimd
    def _(pool):
        pool.wait_ge(ident_loaded, 16)
        nc.gpsimd.tensor_copy(ident16[:, :], ident[:, :]).then_inc(ident16_ready, 1)
        nc.gpsimd.tensor_copy(identh[:, :], ident[:, :]).then_inc(ident16_ready, 1)
        pool.wait_ge(prep, MAT_MAX_READY)
        pool.wait_ge(ident16_ready, 2)
        nc.gpsimd.partition_all_reduce(mat_max[:, 1, :], mat_max[:, 0, :], P, RMAX).then_inc(mat_reduced, 1)
        pool.wait_ge(down_ready, 1)
        pool.wait_ge(mat_reduced, 1)
        nc.gpsimd.partition_all_reduce(down_max[:, 1, :], down_max[:, 0, :], P, RMAX).then_inc(mat_reduced, 1)

        def qk_sum(k, t):
            pool.wait_ge(rope_ready, BLK * k + t + 1)
            if t >= 2 or not (isinstance(k, int) and k == 0):
                pool.wait_ge(rem_ready, BLK * k + t - 1)
            nc.gpsimd.tensor_tensor(qk_rot[:, t % 2, :], rot_c[:, t % 2, :], rot_s[:, t % 2, :],
                                    ALU.add).then_inc(qk_ready, 1)

        def lo_part(k, t):
            pool.wait_ge(part_mid, BLK * k + t + 1)
            nc.gpsimd.tensor_tensor(parts[:, t % 2, 2, :], qk_rem[:, t % 2, :], parts[:, t % 2, 1, :],
                                    ALU.subtract).then_inc(parts_ready, 1)

        def h_lo(k, j):
            pool.wait_ge(hhi_ready, HT * k + j + 1)
            nc.gpsimd.tensor_tensor(hT[:, 1, j, :], h32[:, j % 2, :], hT[:, 0, j, :], ALU.subtract).then_inc(hlo_ready, 1)

        def block_a(k):
            qk_sum(k, 0)
            qk_sum(k, 1)
            lo_part(k, 0)
            qk_sum(k, 2)
            lo_part(k, 1)
            qk_sum(k, 3)
            h_lo(k, 0)
            h_lo(k, 1)
            lo_part(k, 2)
            h_lo(k, 2)
            lo_part(k, 3)
            for j in range(3, HT):
                h_lo(k, j)

        block_a(0)
        with pool.Fori(1, NBLK) as k:
            block_a(k)

        pool.wait_ge(down_full, BLK * NBLK)
        pool.wait_ge(y_ready, BLK * NBLK)
        pool.wait_ge(y_out, 16 * NBLK)
        pool.wait_ge(staged_out, 16 * N_STAGED * NBLK)
        nc.gpsimd.memset(k_op[ROWS:ROWS + 32, :, :], 1.0).then_inc(b_const, 1)
        pool.wait_ge(b_const, 1)
        nc.gpsimd.memset(v_op[:, :, :, DH:DH + 1], 1.0).then_inc(b_const, 1)
        pool.wait_ge(b_const, 2)
        nc.gpsimd.memset(v_op[:, :, :, DH + 1:32], 0.0).then_inc(b_const, 1)
        pool.wait_ge(b_const, 3)
        nc.gpsimd.memset(stab[:, :, :], 0.0).then_inc(b_const, 1)
        pool.wait_ge(b_const, 4)
        nc.gpsimd.memset(zero[:, :], 0.0).then_inc(b_const, 1)
        pool.wait_ge(b_const, 5)

        def split_max(h, first):
            n = 4 * h
            pool.wait_ge(max_ready, h + 1)
            if not first:
                pool.wait_ge(stab_loaded, 16 * h)
            nc.gpsimd.tensor_tensor(stab[:, 0, :], neg_max[:, :], zero[:, :], ALU.add).then_inc(stab_step, 1)
            pool.wait_ge(stab_step, n + 1)
            nc.gpsimd.tensor_tensor(neg_rem[:, :], neg_max[:, :], stab[:, 0, :], ALU.subtract).then_inc(stab_step, 1)
            pool.wait_ge(stab_step, n + 2)
            nc.gpsimd.tensor_tensor(stab[:, 1, :], neg_rem[:, :], zero[:, :], ALU.add).then_inc(stab_step, 1)
            pool.wait_ge(stab_step, n + 3)
            nc.gpsimd.tensor_tensor(stab[:, 2, :], neg_rem[:, :], stab[:, 1, :], ALU.subtract).then_inc(stab_step, 1)

        split_max(0, True)
        with pool.Fori(1, HEADS) as h:
            split_max(h, False)

    @block.vector
    def _(dve):
        count = [0]

        def step_done(ins):
            count[0] += 1
            ins.then_inc(prep, 1)

        def wait_prep():
            dve.wait_ge(prep, count[0])

        def powers(dst_pow, dst_inv, src):
            step_done(nc.vector.tensor_scalar(dst_pow.bitcast(I32), src.bitcast(I32), EXPONENT, None, ALU.bitwise_and))
            wait_prep()
            step_done(nc.vector.tensor_scalar(dst_inv.bitcast(I32), dst_pow.bitcast(I32), -1.0, TWO_EXPONENTS, ALU.mult, ALU.add))

        NQ = 3 * D // P
        dve.wait_ge(w_loaded, 80)
        step_done(nc.vector.tensor_scalar(nat["g"], nat["gi"], 1.0, None, ALU.mult))
        step_done(nc.vector.tensor_scalar(nat["u"], nat["ui"], 1.0, None, ALU.mult))
        step_done(nc.vector.tensor_scalar(nat["d"], nat["di"], 1.0, None, ALU.mult))
        wait_prep()
        for nm, r0, n in (("qkv", 0, NQ), ("g", NQ, HT), ("u", NQ + HT, HT)):
            step_done(nc.vector.tensor_reduce(largest[:, r0:r0 + n], nat[nm], AX.X, ALU.max, apply_absolute_value=True))
        wait_prep()
        step_done(nc.vector.tensor_reduce(mat_max[:, 0, 0:1], largest[:, 0:2 * D // P], AX.X, ALU.max))
        step_done(nc.vector.tensor_reduce(mat_max[:, 0, 1:2], largest[:, 2 * D // P:NQ], AX.X, ALU.max))
        assert count[0] == MAT_MAX_READY
        step_done(nc.vector.tensor_scalar(row_max1[:, :], largest[:, NQ:NROW], 1.0, None, ALU.max))
        wait_prep()
        powers(pow_gu[:, :], inv_gu[:, :], row_max1[:, :])
        wait_prep()
        step_done(nc.vector.tensor_scalar(scale_gu[:, :], inv_gu[:, :], W_SCALE, None, ALU.mult))
        step_done(nc.vector.tensor_scalar(gate_fix[:, :], pow_gu[:, 0:HT], QUANT_SCALE / (W_SCALE * X_SCALE), None, ALU.mult))
        step_done(nc.vector.tensor_scalar(h_fix[:, :], inv_gu[:, 0:HT], QUANT_SCALE * H_SCALE / (W_SCALE * X_SCALE), None,
                                          ALU.mult))
        step_done(nc.vector.tensor_tensor(pow_prod[:, :], pow_gu[:, 0:HT], pow_gu[:, HT:2 * HT], ALU.mult))
        wait_prep()
        step_done(nc.vector.tensor_scalar(h_inv[:, :], pow_prod[:, :], 1.0 / H_SCALE, None, ALU.mult))
        dve.wait_ge(mat_reduced, 1)
        step_done(nc.vector.tensor_scalar(mat_max[:, 2, :], mat_max[:, 1, :], 1e-30, None, ALU.max))
        wait_prep()
        powers(pow_m[:, 0:2], inv_m[:, 0:2], mat_max[:, 2, :])
        wait_prep()
        step_done(nc.vector.tensor_scalar(scale_m[:, 0:2], inv_m[:, 0:2], W_SCALE, None, ALU.mult))
        step_done(nc.vector.tensor_scalar(fix_m[:, 0:2], pow_m[:, 0:2], 1.0 / (W_SCALE * X_SCALE), None, ALU.mult))
        assert count[0] == SCALES_READY, count
        wait_prep()
        for r in range(NROW):
            src, sc = nat_row(r)
            dve.wait_ge(hi_ready, r + 1)
            nc.vector.scalar_tensor_tensor(nat16[:, 1, r, :], src, sc, nat16[:, 0, r, :], ALU.mult,
                                           ALU.subtract).then_inc(lo_ready, 1)
        dve.wait_ge(tables_loaded, 32)
        step_done(nc.vector.tensor_scalar(cos_t[:, :, :], cos_t[:, :, :], fix_m[:, 0:1], None, ALU.mult))
        step_done(nc.vector.tensor_scalar(sin_t[:, :, :], sin_t[:, :, :], fix_m[:, 0:1], None, ALU.mult))
        dve.wait_ge(wd_saved, 1 + HT)
        nc.vector.tensor_reduce(down_max[:, 0, :], wdT32, AX.XY, ALU.max, apply_absolute_value=True).then_inc(down_ready, 1)
        dve.wait_ge(mat_reduced, 2)
        step_done(nc.vector.tensor_scalar(down_max[:, 2, :], down_max[:, 1, :], 1e-30, None, ALU.max))
        wait_prep()
        powers(pow_m[:, 2:3], inv_m[:, 2:3], down_max[:, 2, :])
        wait_prep()
        step_done(nc.vector.tensor_scalar(scale_m[:, 2:3], inv_m[:, 2:3], W_SCALE, None, ALU.mult))
        step_done(nc.vector.tensor_scalar(fix_m[:, 2:3], pow_m[:, 2:3], QUANT_SCALE / W_SCALE, None, ALU.mult))
        wait_prep()
        step_done(nc.vector.tensor_scalar(wdT[:, 0], wdT32, scale_m[:, 2:3], None, ALU.mult))
        wait_prep()
        step_done(nc.vector.scalar_tensor_tensor(wdT[:, 1], wdT32, scale_m[:, 2:3], wdT[:, 0], ALU.mult, ALU.subtract))
        assert count[0] == DOWN_SPLIT, count
        wait_prep()

        def row_stats(k):
            dve.wait_ge(x_loaded, 16 * (k + 1))
            for t in range(BLK):
                ins = nc.vector.bn_stats(stats[:, t, :], x_ln[:, t, :])
            ins.then_inc(ln_step, 1)
            dve.wait_ge(ln_step, LN_STEPS * k + 1)

        def ln_steps(k, n):
            count = [LN_STEPS * k + n]

            def done(ins):
                count[0] = count[0] + 1
                ins.then_inc(ln_step, 1)

            def wait():
                dve.wait_ge(ln_step, count[0])

            return done, wait

        def ln_seed(k):
            done, wait = ln_steps(k, 1)
            for t in range(BLK):
                ins = nc.vector.bn_aggr(mv[:, t, :], stats[:, t, :])
            done(ins)
            wait()
            done(nc.vector.tensor_scalar(ve[:, :], mv[:, :, 1], EPS, None, ALU.add))
            wait()
            done(nc.vector.tensor_scalar(seed[:, :], ve[:, :].bitcast(I32), 1, None, ALU.logical_shift_right))
            wait()
            done(nc.vector.tensor_scalar(rs[:, 0, :].bitcast(I32), seed[:, :], -1.0, float(0x5F3759DF), ALU.mult, ALU.add))
            wait()

        def ln_newton(k, r):
            done, wait = ln_steps(k, 5 + 4 * r)
            done(nc.vector.tensor_tensor(nt_a[:, r, :], rs[:, r, :], rs[:, r, :], ALU.mult))
            wait()
            done(nc.vector.tensor_tensor(nt_b[:, r, :], nt_a[:, r, :], ve[:, :], ALU.mult))
            wait()
            done(nc.vector.tensor_scalar(nt_a[:, r, :], nt_b[:, r, :], -0.5, 1.5, ALU.mult, ALU.add))
            wait()
            done(nc.vector.tensor_tensor(rs[:, r + 1, :], rs[:, r, :], nt_a[:, r, :], ALU.mult))
            wait()

        def normalise(k, first):
            if not first:
                dve.wait_ge(xT_full, KT * k)
            for t in range(BLK):
                ins = nc.vector.tensor_scalar(xn[:, t, :], x_ln[:, t, :], mv[:, t, 0:1], rs[:, 3, t:t + 1],
                                              ALU.subtract, ALU.mult)
            ins.then_inc(xn_ready, 1)

        def rope(k, t):
            dve.wait_ge(pair_full, PAIRS * k + t + 1)
            if t >= 2 or not (isinstance(k, int) and k == 0):
                dve.wait_ge(qk_ready, BLK * k + t - 1)
            G = 2 * H
            a, b = PAIR_BANK[t], PAIR_BANK[t] + 1
            qk = bank(a).rearrange("p (g s f) -> p g s f", g=G, s=2)
            rc = rot_c[:, t % 2, :].rearrange("p (g s f) -> p g s f", g=G, s=2)
            rsn = rot_s[:, t % 2, :].rearrange("p (g s f) -> p g s f", g=G, s=2)
            tile = k * BLK + t
            HF = DH // 2
            cos = cos_t[:, bass.ds(tile, 1), :].rearrange("p a f -> p (a f)")
            sin = sin_t[:, bass.ds(tile, 1), :].rearrange("p a f -> p (a f)")
            for s in range(2):
                nc.vector.tensor_tensor(rc[:, :, s, :], qk[:, :, s, :], cos.unsqueeze(1).to_broadcast([P, G, HF]), ALU.mult)
            for s in range(2):
                ins = nc.vector.tensor_tensor(rsn[:, :, s, :], qk[:, :, 1 - s, :],
                                              sin[:, s * HF:(s + 1) * HF].unsqueeze(1).to_broadcast([P, G, HF]), ALU.mult)
            ins.then_inc(rope_ready, 1)
            nc.vector.tensor_scalar(v_all[:, bass.ds(tile, 1), :, :].rearrange("p a h d -> p (a h d)"), bank(b, D), fix_m[:, 1:2],
                                    None, ALU.mult).then_inc(pair_used, 1)

        def mid_part(k, t):
            dve.wait_ge(part_hi, BLK * k + t + 1)
            if t >= 2 or not (isinstance(k, int) and k == 0):
                dve.wait_ge(parts_ready, BLK * k + t - 1)
            nc.vector.tensor_tensor(qk_rem[:, t % 2, :], qk_rot[:, t % 2, :], parts[:, t % 2, 0, :],
                                    ALU.subtract).then_inc(rem_ready, 1)
            dve.wait_ge(rem_ready, BLK * k + t + 1)
            nc.vector.tensor_copy(parts[:, t % 2, 1, :], qk_rem[:, t % 2, :]).then_inc(part_mid, 1)

        def gate_up(k, j):
            dve.wait_ge(silu_ready, HT * k + j + 1)
            dve.wait_ge(pair_full, PAIRS * k + BLK + j + 1)
            if j >= 2 or not (isinstance(k, int) and k == 0):
                dve.wait_ge(hlo_ready, HT * k + j - 1)
            nc.vector.scalar_tensor_tensor(h32[:, j % 2, :], bank(PAIR_BANK[BLK + j] + 1), h_fix[:, j:j + 1], silu[:, j % 2, :],
                                           ALU.mult, ALU.mult).then_inc(pair_used, 1)

        def add_x(k, t):
            dve.wait_ge(down_full, BLK * k + t + 1)
            if t == 0:
                dve.wait_ge(xres_loaded, 16 * (k + 1))
                if not (isinstance(k, int) and k == 0):
                    dve.wait_ge(y_out, 16 * k)
            nc.vector.scalar_tensor_tensor(y_blk[:, t, :], bank(DOWN_BANK[t], D), fix_m[:, 2:3], x_res[:, t, :], ALU.mult,
                                           ALU.add).then_inc(y_ready, 1)

        def x_lo(k, c):
            dve.wait_ge(xT_saved, KT * k + c + 1)
            nc.vector.scalar_tensor_tensor(xnT[:, 1, c, :], bank(c), X_SCALE, xnT[:, 0, c, :], ALU.mult,
                                           ALU.subtract).then_inc(xlo_ready, 1)

        def block_a(k, last):
            rope(k, 0)
            rope(k, 1)
            rope(k, 2)
            mid_part(k, 0)
            rope(k, 3)
            mid_part(k, 1)
            gate_up(k, 0)
            if not last:
                row_stats(k + 1)
            gate_up(k, 1)
            if not last:
                ln_seed(k + 1)
            mid_part(k, 2)
            gate_up(k, 2)
            if not last:
                ln_newton(k + 1, 0)
            mid_part(k, 3)
            gate_up(k, 3)
            if not last:
                ln_newton(k + 1, 1)
                ln_newton(k + 1, 2)
                normalise(k + 1, False)
            for j in range(4, HT):
                gate_up(k, j)
            if not last:
                for c in range(KT):
                    x_lo(k + 1, c)
            for t in range(BLK):
                add_x(k, t)

        row_stats(0)
        ln_seed(0)
        for r in range(3):
            ln_newton(0, r)
        normalise(0, True)
        dve.wait_ge(wt_saved, WG)
        for c in range(KT):
            x_lo(0, c)
        block_a(0, False)
        with dve.Fori(1, NBLK - 1) as k:
            block_a(k, False)
        block_a(NBLK - 1, True)

        dve.wait_ge(b_const, 5)

        def step(c, i):
            hl, t = divmod(c, TILES)
            h = head_of(c, TILES)
            if h is not None:
                dve.wait_ge(s1_used, 2 * TILES * (h + 1 + SLOTS * i))
                if h >= 1:
                    dve.wait_ge(stab_step, 4 * (h + SLOTS * i))
                nc.vector.tensor_reduce(neg_max[:, :], row_max[:, h % 2, :, :], AX.X, ALU.max, negate=True).then_inc(max_ready, 1)
            h = head_of(c, VCOPY_AT)
            if h is not None:
                if h >= 2:
                    dve.wait_ge(pv_done, TILES * (h - 1 + SLOTS * i))
                hh = h + SLOTS * i
                src = v_all[:, bass.ds(sequence_of(hh) * TILES, TILES), bass.ds(hh & (H - 1), 1), :].rearrange("p t a d -> p t (a d)")
                nc.vector.tensor_scalar(v_op[:, h % 2, :, 0:DH], src, 1.0, None, ALU.mult).then_inc(v_ready, 1)
            h = head_of(c, NORM_AT)
            if h is not None:
                g = TILES * h + TURN_AT
                dve.wait_ge(s2_used, items_before(g) + 1 + HEAD_ITEMS * SLOTS * i)
                turned = oT_sb[:, :].rearrange("p (n j d) -> p j n d", n=4, j=4)
                if h >= 1:
                    dve.wait_ge(o_ready, h + SLOTS * i)
                nc.vector.reciprocal(inv_sum[:, :, :], turned[:, :, :, DH]).then_inc(sum_inv, 1)
                dve.wait_ge(sum_inv, h + 1 + SLOTS * i)
                hh = h + SLOTS * i
                dst = o_all[:, bass.ds(sequence_of(hh) * TILES, TILES), bass.ds(hh & (H - 1), 1), :].rearrange(
                    "p (j n) a d -> p j n (a d)", j=4)
                nc.vector.tensor_tensor(dst, turned[:, :, :, 0:DH], inv_sum[:, :, :].unsqueeze(3).to_broadcast([P, 4, 4, DH]),
                                        ALU.mult).then_inc(o_ready, 1)
            if c < N1:
                for half in range(2):
                    dve.wait_ge(s1_full, 2 * c + half + 1 + 2 * UNROLL * i)
                    nc.vector.tensor_reduce(row_max[:, hl % 2, t, half:half + 1], psum[:, 2 * half * BANK:(2 * half + 2) * BANK],
                                            AX.X, ALU.max).then_inc(s1_used, 1)

        run_steps(dve, step)

        dve.wait_ge(o_ready, HEADS)

        def gather(n, j, first):
            k = 2 * n + j
            if not first:
                dve.wait_ge(cT_full, KT * (k - 1))
            nc.vector.tensor_scalar(o_blk[:, j, :, :], o_all[:, bass.ds(k * BLK, BLK), :, :].rearrange("p t h d -> p t (h d)"),
                                    1.0, None, ALU.mult).then_inc(c_gathered, 1)

        def add_y(n, j, first):
            k = 2 * n + j
            dve.wait_ge(yin_loaded[j], 16 * (n + 1))
            if not first:
                dve.wait_ge(res_out[j], 16 * n)
            for u in range(2):
                dve.wait_ge(proj_full, 2 * k + u + 1)
                nc.vector.tensor_tensor(res[:, j, 2 * u:2 * u + 2, :], bank(4 + 2 * j + u).rearrange("p (t d) -> p t d", t=2),
                                        y_in[:, j, 2 * u:2 * u + 2, :], ALU.add).then_inc(res_ready, 1)

        for j in range(2):
            gather(0, j, True)
        for j in range(2):
            add_y(0, j, True)
        with dve.Fori(1, NBLK // 2) as n:
            for j in range(2):
                gather(n, j, False)
            for j in range(2):
                add_y(n, j, False)

    keep.close()


def kernel(**inputs):
    import numpy as np
    import concourse.bacc as bacc
    from concourse.bass_utils import run_bass_kernel_spmd

    xs = np.ascontiguousarray(inputs["L0_attn_x"])
    nb, L, D = xs.shape
    n_tok = nb * L
    half = DH // 2
    inv_freq = (np.float32(1.0) / np.power(np.float32(10000.0), np.arange(half, dtype=np.float32) / np.float32(half))).astype(np.float32)
    ang = np.arange(L, dtype=np.float32)[:, None] * inv_freq[None, :]
    cos, sin = np.cos(ang).astype(np.float32), np.sin(ang).astype(np.float32)
    cos = np.tile(cos, (nb, 1)).reshape(n_tok // P, P, half).transpose(1, 0, 2)
    sin = np.tile(np.concatenate([-sin, sin], axis=1), (nb, 1)).reshape(n_tok // P, P, DH).transpose(1, 0, 2)

    arrays = {
        "in_x": xs.reshape(n_tok, D),
        "in_w_qkv": np.ascontiguousarray(inputs["L0_attn_w_qkv"]),
        "in_w_out": np.ascontiguousarray(inputs["L0_attn_w_out"]),
        "in_w_gate": np.ascontiguousarray(inputs["L0_ffn_w_gate"]),
        "in_w_up": np.ascontiguousarray(inputs["L0_ffn_w_up"]),
        "in_w_down": np.ascontiguousarray(inputs["L0_ffn_w_down"]),
        "in_cos": np.ascontiguousarray(cos),
        "in_sin": np.ascontiguousarray(sin),
        "in_ident": np.eye(P, dtype=np.float32),
    }
    nc = bacc.Bacc("TRN2", target_bir_lowering=False, num_devices=1)
    ins = [nc.dram_tensor(n, a.shape, mybir.dt.from_np(a.dtype), kind="ExternalInput").ap() for n, a in arrays.items()]
    out = nc.dram_tensor("out_y", (n_tok, D), F32, kind="ExternalOutput").ap()
    y_dram = nc.dram_tensor("y_dram", (n_tok, D), F32, kind="Internal").ap()
    qk_dram = nc.dram_tensor("qk_dram", (2, PARTS, D, n_tok), BF16, kind="Internal").ap()
    layer_program(nc, *ins, out, y_dram, qk_dram)
    r = run_bass_kernel_spmd(nc, [arrays], core_ids=[0])
    return r.results[0]["out_y"].reshape(nb, L, D)
```

```python
from contextlib import ExitStack

import concourse.bass as bass
from concourse import mybir

F32 = mybir.dt.float32
BF16 = mybir.dt.bfloat16
F16 = mybir.dt.float16
I32 = mybir.dt.int32
ALU = mybir.AluOpType
ACT = mybir.ActivationFunctionType
AX = mybir.AxisListType
RMAX = bass.bass_isa.ReduceOp.max

P = 128
DH = 16
BANK = 512
TILES = 16
BLK = 4
PARTS = 3
Q_PART = [0, 1, 2, 0, 1, 0]
K_PART = [0, 0, 0, 1, 1, 2]
ROWS = len(Q_PART) * DH
SLOTS = 4
LAG = 3
RING = 3
UNROLL = SLOTS * TILES
PRODUCTS = [(0, 0), (0, 1), (1, 0)]
EXACT_PRODUCTS = [(0, 0), (1, 0)]
EPS = 1e-5
QUANT_SCALE = 1.0 / 127.0
X_SCALE = 2.0 ** 11
W_SCALE = 2.0 ** 13
H_SCALE = 2.0 ** 10
EXACT_INT = 2.0 ** 11
EXPONENT = 0x7F800000
TWO_EXPONENTS = float(254 << 23)


def layer_program(nc, x, w_qkv, w_out, w_gate, w_up, w_down, cos_tab, sin_tab, ident_in, out, y_dram, qk_dram):
    TOKENS, D = x.shape
    HID = w_gate.shape[0]
    H = D // DH
    KT = D // P
    HT = HID // P
    NT = TOKENS // P
    NBLK = NT // BLK
    HEADS = (TOKENS // (TILES * P)) * H
    SCALE = float(DH) ** -0.5
    assert D == 256 and KT == 2 and HEADS % SLOTS == 0 and HEADS > H

    x_blocks = x.rearrange("(k t p) d -> k p t d", p=P, t=BLK)
    y_blocks = y_dram.rearrange("(k t p) d -> k p t d", p=P, t=BLK)
    out_blocks = out.rearrange("(k t p) d -> k p t d", p=P, t=BLK)

    keep = ExitStack()

    def sb(stack, name, shape, dt=F32):
        return stack.enter_context(nc.sbuf_tensor(name, shape, dt))

    def sem(name):
        return keep.enter_context(nc.semaphore(name))

    PAIRS = BLK + HT
    PAIR_BANK = [6, 4, 2, 6, 4, 2, 6, 4, 2, 4]
    DOWN_BANK = [6, 7, 2, 3]
    H_BUFS = 4
    PREFIX = 3
    LN_STEPS = 5 + 3 * 4
    N_STAGED = 2 * KT

    ident = sb(keep, "ident", [P, P])
    ident16 = sb(keep, "ident16", [P, P], BF16)
    identh = sb(keep, "identh", [P, P], F16)
    v_space = sb(keep, "v_space", [P, max(NT * D, (3 * D * D + D * D + 5 * HID * D + (3 * D + 2 * HID) * D) // P)])
    v_all = v_space[:, 0:NT * D].rearrange("p (t h d) -> p t h d", h=H, d=DH)
    woT = sb(keep, "woT", [P, KT, D])
    sa = ExitStack()
    WCOLS = 3 * KT * D + 2 * KT * HID
    w16 = sb(sa, "w16", [P, 2, WCOLS], F16)
    o0 = 0
    wqkvT = w16[:, :, o0:o0 + KT * 3 * D].rearrange("p a (k e) -> p a k e", k=KT)
    o0 += KT * 3 * D
    wgT = w16[:, :, o0:o0 + KT * HID].rearrange("p a (k e) -> p a k e", k=KT)
    o0 += KT * HID
    wuT = w16[:, :, o0:o0 + KT * HID].rearrange("p a (k e) -> p a k e", k=KT)
    wdT = sb(sa, "wdT", [P, 2, HT, D], F16)
    NROW = 3 * D // P + 2 * HT
    largest = sb(sa, "largest", [P, NROW])
    row_max1 = sb(sa, "row_max1", [P, 2 * HT])
    pow_gu = sb(sa, "pow_gu", [P, 2 * HT])
    inv_gu = sb(sa, "inv_gu", [P, 2 * HT])
    scale_gu = sb(sa, "scale_gu", [P, 2 * HT])
    gate_fix = sb(sa, "gate_fix", [P, HT])
    h_fix = sb(sa, "h_fix", [P, HT])
    pow_prod = sb(sa, "pow_prod", [P, HT])
    h_inv = sb(sa, "h_inv", [P, HT])
    lo_max = sb(sa, "lo_max", [P, 3, 2])
    gu_max = sb(sa, "gu_max", [P, 1])
    mat_max = sb(sa, "mat_max", [P, 3, 2])
    down_max = sb(sa, "down_max", [P, 3, 1])
    pow_m = sb(sa, "pow_m", [P, 3])
    inv_m = sb(sa, "inv_m", [P, 3])
    scale_m = sb(sa, "scale_m", [P, 3])
    fix_m = sb(sa, "fix_m", [P, 3])
    cos_t = sb(sa, "cos_t", [P, NT, DH // 2])
    sin_t = sb(sa, "sin_t", [P, NT, DH])
    x_ln = sb(sa, "x_ln", [P, BLK, D])
    x_res = sb(sa, "x_res", [P, BLK, D])
    stats = sb(sa, "stats", [P, BLK, 6])
    mv = sb(sa, "mv", [P, BLK, 2])
    ve = sb(sa, "ve", [P, BLK])
    seed = sb(sa, "seed", [P, BLK], I32)
    rs = sb(sa, "rs", [P, 4, BLK])
    nt_a = sb(sa, "nt_a", [P, 3, BLK])
    nt_b = sb(sa, "nt_b", [P, 3, BLK])
    xn = sb(sa, "xn", [P, BLK, D])
    xnT = sb(sa, "xnT", [P, 2, KT, BLK * P], F16)
    rot_c = sb(sa, "rot_c", [P, 2, 2 * D])
    rot_s = sb(sa, "rot_s", [P, 2, 2 * D])
    qk_rot = sb(sa, "qk_rot", [P, BLK, 2 * D])
    qk_rem = sb(sa, "qk_rem", [P, 2, 2 * D])
    parts = sb(sa, "parts", [P, BLK, PARTS, 2 * D], BF16)
    staged = sb(sa, "staged", [P, PARTS, 2 * KT, BLK * P], BF16)
    silu = sb(sa, "silu", [P, 2, BANK])
    h32 = sb(sa, "h32", [P, H_BUFS, BANK])
    hT = sb(sa, "hT", [P, 2, HT, BLK * P], F16)
    y_blk = sb(sa, "y_blk", [P, BLK, D])
    n0 = 0
    nat = {}
    for nm, rows, cols in (("qkv", 3 * D, D), ("o", D, D), ("d", D, HID), ("gi", HID, D), ("ui", HID, D), ("di", D, HID),
                           ("dT", HID, D)):
        n = rows // P * cols
        nat[nm] = v_space[:, n0:n0 + n]
        if nm.endswith("i"):
            nat[nm] = nat[nm].bitcast(I32)
        nat[nm] = nat[nm].rearrange("p (t c) -> p t c", c=cols)
        n0 += n
    n16 = NROW * D // 2
    nat16 = v_space[:, n0:n0 + 2 * n16].bitcast(F16).rearrange("p (a t c) -> p a t c", a=2, c=D)
    n0 += 2 * n16
    wdT32 = nat["dT"]
    sa.close()

    sB = ExitStack()
    o_all = v_all
    q_op = sb(sB, "q_op", [P, SLOTS, TILES * P], BF16)
    k_op = sb(sB, "k_op", [P, SLOTS, TILES * P], BF16)
    probs = sb(sB, "probs", [P, 2, TILES * P])
    v_op = sb(sB, "v_op", [P, 2, TILES, 32])
    row_max = sb(sB, "row_max", [P, 2, TILES, 2])
    neg_max = sb(sB, "neg_max", [P, TILES])
    neg_rem = sb(sB, "neg_rem", [P, TILES])
    zero = sb(sB, "zero", [P, TILES])
    stab = sb(sB, "stab", [P, P // TILES, TILES], BF16)
    stabT = sb(sB, "stabT", [PARTS * TILES, P], BF16)
    acc_sb = sb(sB, "acc_sb", [P, BANK])
    oT_sb = sb(sB, "oT_sb", [P, BANK])
    inv_sum = sb(sB, "inv_sum", [P, 4, 4])
    o_blk = sb(sB, "o_blk", [P, 2, BLK, D])
    oT = sb(sB, "oT", [P, 2, KT, BLK * P])
    y_in = sb(sB, "y_in", [P, 2, BLK, D])
    res = sb(sB, "res", [P, 2, BLK, D])
    sB.close()

    psum = keep.enter_context(nc.psum_tensor("psum", [P, 8 * BANK], F32))

    def bank(n, cols=BANK):
        return psum[:, n * BANK:n * BANK + cols]

    wqkv_loaded = sem("wqkv_loaded")
    wgate_loaded = sem("wgate_loaded")
    wup_loaded = sem("wup_loaded")
    wdown_loaded = sem("wdown_loaded")
    wout_loaded = sem("wout_loaded")
    down_float = sem("down_float")
    ident_loaded = sem("ident_loaded")
    tables_loaded = sem("tables_loaded")
    ident16_ready = sem("ident16_ready")
    prep = sem("prep")
    mat_reduced = sem("mat_reduced")
    hi_ready = sem("hi_ready")
    lo_ready = sem("lo_ready")
    down_ready = sem("down_ready")
    lo_bits_ready = sem("lo_bits_ready")
    wd_full = sem("wd_full")
    wd_saved = sem("wd_saved")
    wt_full = sem("wt_full")
    wt_saved = sem("wt_saved")
    x_loaded = sem("x_loaded")
    xres_loaded = sem("xres_loaded")
    ln_step = sem("ln_step")
    xn_ready = sem("xn_ready")
    xT_full = sem("xT_full")
    xT_saved = sem("xT_saved")
    xlo_ready = sem("xlo_ready")
    pair_full = sem("pair_full")
    pair_used = sem("pair_used")
    silu_ready = sem("silu_ready")
    hhi_ready = sem("hhi_ready")
    hlo_ready = sem("hlo_ready")
    rope_ready = sem("rope_ready")
    qk_ready = sem("qk_ready")
    part_hi = sem("part_hi")
    part_hi_v = sem("part_hi_v")
    rem_ready = sem("rem_ready")
    part_mid = sem("part_mid")
    parts_ready = sem("parts_ready")
    partsT_full = sem("partsT_full")
    partsT_saved = sem("partsT_saved")
    staged_out = sem("staged_out")
    down_full = sem("down_full")
    y_ready = sem("y_ready")
    y_out = sem("y_out")
    b_const = sem("b_const")
    qk_loaded = [sem(f"qk_loaded{s}") for s in range(SLOTS)]
    stab_loaded = sem("stab_loaded")
    s1_full = sem("s1_full")
    s1_used = sem("s1_used")
    s2_full = sem("s2_full")
    s2_used = sem("s2_used")
    pv_done = sem("pv_done")
    acc_saved = sem("acc_saved")
    v_ready = sem("v_ready")
    max_ready = sem("max_ready")
    stab_step = sem("stab_step")
    sum_inv = sem("sum_inv")
    o_ready = sem("o_ready")
    c_gathered = sem("c_gathered")
    cT_full = sem("cT_full")
    cT_saved = sem("cT_saved")
    proj_full = sem("proj_full")
    yin_loaded = [sem("yin_loaded0"), sem("yin_loaded1")]
    res_ready = sem("res_ready")
    res_out = [sem("res_out0"), sem("res_out1")]

    wt_blocks = [(a, r0 + j, k) for a in range(2) for r0, n in ((0, 3 * D // P), (3 * D // P, HT), (3 * D // P + HT, HT))
                 for k in range(KT) for j in range(n)]
    WG = len(wt_blocks) // 8

    N1 = HEADS * TILES
    FIRST2 = TILES + LAG
    STAB_AT = TILES + 1
    SAVE_AT = FIRST2 + TILES + 1
    TURN_AT = SAVE_AT + 1
    NORM_AT = TURN_AT + 1
    VCOPY_AT = 10
    FIRST_C = N1 + 2
    STEPS_B = N1 + (NORM_AT - TILES) + 1
    HEAD_ITEMS = 4 * TILES + 2
    assert HEAD_ITEMS % RING == 0
    PRO = NORM_AT
    BODIES = (N1 - PRO) // UNROLL

    def head_of(g, at):
        h, r = divmod(g - at, TILES)
        return h if r == 0 and 0 <= h < HEADS else None

    def sequence_of(h):
        n = h >> (H.bit_length() - 1)
        if not isinstance(h, int):
            n.max_val = HEADS // H - 1
        return n

    def before(g, at):
        return min(max((g - at + TILES - 1) // TILES, 0), HEADS)

    def items_before(g):
        return 4 * min(max(g - FIRST2, 0), N1) + before(g, STAB_AT) + before(g, TURN_AT)

    def extra_items(g):
        return (head_of(g, STAB_AT) is not None) + (head_of(g, TURN_AT) is not None)

    def run_steps(eng, step):
        for c in range(PRO):
            step(c, 0)
        if BODIES:
            with eng.Fori(0, BODIES) as i:
                for c in range(PRO, PRO + UNROLL):
                    step(c, i)
        for c in range(PRO + UNROLL * BODIES, STEPS_B):
            step(c, 0)

    MAT_MAX_READY, SCALES_READY, DOWN_SPLIT, LO_MAX_READY = 5, 18, 29, 31

    NQ = 3 * D // P
    NSPLIT = 2 + 2 * HT

    def split_unit(n):
        if n < 2:
            r0, r1 = ((0, 2 * D // P), (2 * D // P, NQ))[n]
            return nat["qkv"][:, r0:r1, :], scale_m[:, n:n + 1], slice(r0, r1)
        n -= 2
        return (nat["gi" if n < HT else "ui"][:, n % HT:n % HT + 1, :], scale_gu[:, n:n + 1],
                slice(NQ + n, NQ + n + 1))

    block = keep.enter_context(nc.Block())

    @block.sync
    def _(sp):
        sp.dma_start(ident[:, :], ident_in).then_inc(ident_loaded, 16)
        sp.dma_start(x_ln[:, :, :], x_blocks[0]).then_inc(x_loaded, 16)
        sp.dma_start(nat["qkv"], w_qkv.rearrange("(t p) c -> p t c", p=P)).then_inc(wqkv_loaded, 16)
        sp.dma_start(nat["gi"], w_gate.rearrange("(t p) c -> p t c", p=P)).then_inc(wgate_loaded, 16)
        sp.dma_start(nat["ui"], w_up.rearrange("(t p) c -> p t c", p=P)).then_inc(wup_loaded, 16)
        sp.dma_start(nat["di"], w_down.rearrange("(t p) c -> p t c", p=P)).then_inc(wdown_loaded, 16)
        sp.dma_start(nat["o"], w_out.rearrange("(t p) c -> p t c", p=P)).then_inc(wout_loaded, 16)
        sp.dma_start(cos_t[:, :, :], cos_tab).then_inc(tables_loaded, 16)
        sp.dma_start(sin_t[:, :, :], sin_tab).then_inc(tables_loaded, 16)

        def load_x(k):
            sp.wait_ge(xn_ready, k)
            sp.dma_start(x_ln[:, :, :], x_blocks[k]).then_inc(x_loaded, 16)

        def block_a(k, left):
            if left >= 2:
                load_x(k + 2)
            sp.wait_ge(partsT_saved, BLK * (k + 1))
            for qg in range(2 * KT):
                dst = qk_dram[qg // KT, :, (qg % KT) * P:(qg % KT + 1) * P, bass.ds(k * (BLK * P), BLK * P)]
                sp.dma_start(dst.rearrange("a r n -> r a n"), staged[:, :, qg, :]).then_inc(staged_out, 16)
            sp.wait_ge(y_ready, BLK * (k + 1))
            sp.dma_start(y_blocks[k], y_blk[:, :, :]).then_inc(y_out, 16)
            if left >= 1:
                sp.dma_start(x_res[:, :, :], x_blocks[k + 1]).then_inc(xres_loaded, 16)

        sp.dma_start(x_res[:, :, :], x_blocks[0]).then_inc(xres_loaded, 16)
        load_x(1)
        block_a(0, 2)
        with sp.Fori(1, NBLK - 2) as k:
            block_a(k, 2)
        block_a(NBLK - 2, 1)
        block_a(NBLK - 1, 0)

        sp.wait_ge(staged_out, 16 * N_STAGED * NBLK)
        sp.wait_ge(y_out, 16 * NBLK)
        sp.wait_ge(down_full, BLK * NBLK)

        def load_head(hl, i):
            h = hl + SLOTS * i
            s = hl % SLOTS
            head = (h & (H - 1)) * DH
            tok = sequence_of(h) * (TILES * P)
            src = qk_dram[:, :, bass.ds(head, DH), bass.ds(tok, TILES * P)]
            r = 0
            for n in (3, 2, 1):
                sp.dma_start(q_op[r * DH:(r + n) * DH, s, :], src[0, 0:n]).then_inc(qk_loaded[s], 16)
                r += n
            for r in range(len(K_PART)):
                sp.dma_start(k_op[r * DH:(r + 1) * DH, s, :], src[1, K_PART[r]]).then_inc(qk_loaded[s], 16)

        def load_stab(hl, i):
            h = hl + SLOTS * i
            g = TILES * hl + STAB_AT
            sp.wait_ge(s2_used, items_before(g) + 1 + HEAD_ITEMS * SLOTS * i)
            dst = q_op[ROWS:ROWS + PARTS, hl % SLOTS, :].rearrange("a (t n) -> a t n", t=TILES)
            sp.dma_start(dst, stabT[:, :]).then_inc(stab_loaded, 16)

        def load_y(n, j):
            sp.dma_start(y_in[:, j], y_blocks[2 * n + j]).then_inc(yin_loaded[j], 16)

        load_head(0, 0)
        load_head(1, 0)
        for j in range(2):
            load_y(0, j)
        for hl in range(SLOTS):
            load_stab(hl, 0)
            load_head(hl + 2, 0)
        with sp.Fori(0, HEADS // SLOTS - 2) as i:
            for hl in range(SLOTS, 2 * SLOTS):
                load_stab(hl, i)
                load_head(hl + 2, i)
        for hl in range(HEADS - SLOTS, HEADS):
            load_stab(hl, 0)
            if hl + 2 < HEADS:
                load_head(hl + 2, 0)

        def store_out(n, j):
            sp.wait_ge(res_ready, 2 * (2 * n + j + 1))
            sp.dma_start(out_blocks[2 * n + j], res[:, j]).then_inc(res_out[j], 16)

        with sp.Fori(0, NBLK // 2 - 1) as n:
            for j in range(2):
                store_out(n, j)
                load_y(n + 1, j)
        for j in range(2):
            store_out(NBLK // 2 - 1, j)
        for j in range(2):
            sp.wait_ge(res_out[j], 16 * (NBLK // 2))

    @block.tensor
    def _(pe):
        def turn_x(k, first):
            pe.wait_ge(xn_ready, k + 1)
            if not first:
                pe.wait_ge(partsT_saved, BLK * k)
            for c in range(KT):
                for t in range(BLK):
                    mm = pe.transpose(bank(c)[:, t * P:(t + 1) * P], xn[:, t, c * P:(c + 1) * P], ident[:, :])
                mm.then_inc(xT_full, 1)

        pe.wait_ge(ident_loaded, 16)
        turn_x(0, True)
        pe.wait_ge(wout_loaded, 16)
        pe.wait_ge(down_float, 1)
        pe.wait_ge(xT_saved, KT)
        pe.wait_ge(xlo_ready, KT)
        for k in range(KT):
            for j in range(D // P):
                n = k * (D // P) + j
                mm = pe.transpose(bank(0)[:, n * P:(n + 1) * P], nat["o"][:, j, k * P:(k + 1) * P], ident[:, :])
        mm.then_inc(wd_full, 1)
        for k in range(HT):
            for j in range(D // P):
                n = k * (D // P) + j
                mm = pe.transpose(psum[:, BANK + n * P:BANK + (n + 1) * P], nat["d"][:, j, k * P:(k + 1) * P], ident[:, :])
        mm.then_inc(wd_full, 1)
        pe.wait_ge(ident16_ready, 2)
        pe.wait_ge(hi_ready, NSPLIT)
        pe.wait_ge(lo_ready, NSPLIT)
        for grp in range(WG):
            if grp >= 4:
                pe.wait_ge(wt_saved, grp - 3)
            for j in range(8):
                a, r, c = wt_blocks[8 * grp + j]
                mm = pe.transpose(bank(4 + grp % 4).bitcast(F16)[:, j * P:(j + 1) * P], nat16[:, a, r, c * P:(c + 1) * P],
                                  identh[:, :])
            mm.then_inc(wt_full, 1)
        pe.wait_ge(wt_saved, WG)
        pe.wait_ge(wd_saved, 1 + HT)

        def block_a(k, last, ffn_products):
            def take_pair(u):
                if u < 3:
                    if isinstance(k, int) and k == 0:
                        pass
                    elif u == 0:
                        pe.wait_ge(y_ready, BLK * k - 2)
                    elif u == 1:
                        pe.wait_ge(pair_used, PAIRS * k)
                    else:
                        pe.wait_ge(y_ready, BLK * k)
                else:
                    before_u = max(v for v in range(u) if PAIR_BANK[v] == PAIR_BANK[u])
                    pe.wait_ge(pair_used, PAIRS * k + before_u + 1)
                return PAIR_BANK[u]

            for t in range(BLK):
                if t == 0:
                    pe.wait_ge(xT_saved, KT * (k + 1))
                    pe.wait_ge(xlo_ready, KT * (k + 1))
                a = take_pair(t)
                for dst, e0, e1 in ((bank(a), 0, 2 * D), (bank(a + 1, D), 2 * D, 3 * D)):
                    for c in range(KT):
                        for n, (xp, wp) in enumerate(PRODUCTS):
                            mm = pe.matmul(dst, xnT[:, xp, c, t * P:(t + 1) * P], wqkvT[:, wp, c, e0:e1],
                                           start=(c == 0 and n == 0), stop=(c == KT - 1 and n == 2))
                mm.then_inc(pair_full, 1)
            for j in range(HT):
                a = take_pair(BLK + j)
                for w, dst in ((wgT, a), (wuT, a + 1)):
                    for c in range(KT):
                        for n, (xp, wp) in enumerate(ffn_products):
                            mm = pe.matmul(bank(dst), w[:, wp, c, j * P:(j + 1) * P], xnT[:, xp, c, :],
                                           start=(c == 0 and n == 0), stop=(c == KT - 1 and n == len(ffn_products) - 1))
                mm.then_inc(pair_full, 1)
                if 1 <= j <= BLK:
                    t = j - 1
                    pe.wait_ge(parts_ready, BLK * k + t + 1)
                    if t == 0:
                        pe.wait_ge(xT_saved, KT * (k + 1))
                        pe.wait_ge(xlo_ready, KT * (k + 1))
                    else:
                        pe.wait_ge(partsT_saved, BLK * k + t)
                    turned = psum[:, 0:2 * BANK].bitcast(BF16)
                    for n in range(PARTS * 2 * KT):
                        a, qg = divmod(n, 2 * KT)
                        mm = pe.transpose(turned[:, n * P:(n + 1) * P], parts[:, t, a, qg * P:(qg + 1) * P], ident16[:, :])
                    mm.then_inc(partsT_full, 1)
            if not last:
                turn_x(k + 1, False)

            def down(t, hidden):
                for j in hidden:
                    for n, (hp, wp) in enumerate(ffn_products):
                        mm = pe.matmul(bank(DOWN_BANK[t], D), hT[:, hp, j, t * P:(t + 1) * P], wdT[:, wp, j, :],
                                       start=(j == 0 and n == 0), stop=(j == HT - 1 and n == len(ffn_products) - 1))
                return mm

            for n in (HT - 2, HT - 1, HT):
                pe.wait_ge(hhi_ready, HT * k + n)
                pe.wait_ge(hlo_ready, HT * k + n)
                if n == HT - 1:
                    pe.wait_ge(pair_used, PAIRS * (k + 1) - 1)
                for t in range(PREFIX):
                    mm = down(t, range(HT - 2) if n == HT - 2 else [n - 1])
                    if n == HT:
                        mm.then_inc(down_full, 1)
            for t in range(PREFIX, BLK):
                down(t, range(HT)).then_inc(down_full, 1)

        def blocks_a(ffn_products):
            block_a(0, False, ffn_products)
            with pe.Fori(1, NBLK - 1) as k:
                block_a(k, False, ffn_products)
            block_a(NBLK - 1, True, ffn_products)

        pe.wait_ge(lo_bits_ready, 1)
        lo_bits = pe.value_load(lo_max[0:1, 2, 0:1].bitcast(I32))
        with pe.If(lo_bits == 0):
            blocks_a(EXACT_PRODUCTS)
        with pe.Else():
            blocks_a(PRODUCTS)

        pe.wait_ge(b_const, 5)
        pe.wait_ge(y_ready, BLK * NBLK)
        pe.wait_ge(partsT_saved, BLK * NBLK)

        def turn_o(n, j, first):
            k = 2 * n + j
            pe.wait_ge(c_gathered, k + 1)
            if first and j == 0:
                pe.wait_ge(s1_used, 2 * N1)
            if not first:
                pe.wait_ge(cT_saved, KT * (k - 1))
            for c in range(KT):
                for t in range(BLK):
                    mm = pe.transpose(bank(2 * j + c)[:, t * P:(t + 1) * P], o_blk[:, j, t, c * P:(c + 1) * P], ident[:, :])
                mm.then_inc(cT_full, 1)

        def project(n, j, first):
            k = 2 * n + j
            pe.wait_ge(cT_saved, KT * (k + 1))
            if not first:
                pe.wait_ge(res_ready, 2 * (k - 1))
            for t in range(BLK):
                for c in range(KT):
                    mm = pe.matmul(psum[:, (4 + 2 * j) * BANK + t * D:(4 + 2 * j) * BANK + (t + 1) * D],
                                   oT[:, j, c, t * P:(t + 1) * P], woT[:, c, :], start=(c == 0), stop=(c == KT - 1))
                if t % 2 == 1:
                    mm.then_inc(proj_full, 1)

        def max_half(c, i, half):
            hl, t = divmod(c, TILES)
            if t == 0 and half == 0:
                nd = 16 * (3 + len(K_PART))
                pe.wait_ge(qk_loaded[hl % SLOTS], nd * (hl // SLOTS + 1 + i))
            n = 2 * c + half
            if n >= 2:
                pe.wait_ge(s1_used, n - 1 + 2 * UNROLL * i)
            s = hl % SLOTS
            for j in range(2):
                cols = (2 * half + j) * BANK
                mm = pe.matmul(bank(2 * half + j), q_op[0:ROWS, s, t * P:(t + 1) * P], k_op[0:ROWS, s, cols:cols + BANK],
                               start=True, stop=True)
            mm.then_inc(s1_full, 1)

        def step(c, i):
            item = items_before(c)

            def take_bank(item):
                if item >= RING:
                    pe.wait_ge(s2_used, item - RING + 1 + HEAD_ITEMS * SLOTS * i)
                return 4 + item % RING

            if c < N1:
                max_half(c, i, 0)
            h = head_of(c, STAB_AT)
            if h is not None:
                pe.wait_ge(stab_step, 4 * (h + 1 + SLOTS * i))
                b = take_bank(item)
                pe.transpose(bank(b).bitcast(BF16)[:, 0:P], stab[:, :, :].rearrange("p a t -> p (a t)"),
                             ident16[:, :]).then_inc(s2_full, 1)
                item += 1
            h = head_of(c, TURN_AT)
            if h is not None:
                pe.wait_ge(acc_saved, h + 1 + SLOTS * i)
                b = take_bank(item)
                for n in range(4):
                    mm = pe.transpose(bank(b)[:, n * P:(n + 1) * P], acc_sb[:, n * P:(n + 1) * P], ident[:, :])
                mm.then_inc(s2_full, 1)
                item += 1
            g2 = c - FIRST2
            for j in range(4):
                if j == 2 and c < N1:
                    max_half(c, i, 1)
                if 0 <= g2 < N1:
                    h, t = divmod(g2, TILES)
                    if t == 0 and j == 0:
                        pe.wait_ge(stab_loaded, 16 * (h + 1 + SLOTS * i))
                    b = take_bank(item)
                    pe.matmul(bank(b), k_op[0:ROWS + PARTS, h % SLOTS, t * P:(t + 1) * P],
                              q_op[0:ROWS + PARTS, h % SLOTS, j * BANK:(j + 1) * BANK],
                              start=True, stop=True).then_inc(s2_full, 1)
                    item += 1
            g3 = g2 - 1
            if 0 <= g3 < N1:
                h, t = divmod(g3, TILES)
                if t == 0:
                    pe.wait_ge(v_ready, h + 1 + SLOTS * i)
                    if h >= 1:
                        pe.wait_ge(acc_saved, h + SLOTS * i)
                pe.wait_ge(s2_used, items_before(c - 1) + extra_items(c - 1) + 4 + HEAD_ITEMS * SLOTS * i)
                for j in range(4):
                    mm = pe.matmul(bank(7)[32 * j:32 * j + 32, :], v_op[:, h % 2, t, :], probs[:, g3 % 2, j * BANK:(j + 1) * BANK],
                                   start=(t == 0), stop=(t == TILES - 1), tile_position=(0, 32 * j))
                mm.then_inc(pv_done, 1)

            if c == FIRST_C:
                for j in range(2):
                    turn_o(0, j, True)

        run_steps(pe, step)

        pe.wait_ge(s2_used, items_before(STEPS_B))
        pe.wait_ge(acc_saved, HEADS)
        for j in range(2):
            project(0, j, True)
            turn_o(1, j, False)
        with pe.Fori(1, NBLK // 2 - 1) as n:
            for j in range(2):
                project(n, j, False)
                turn_o(n + 1, j, False)
        for j in range(2):
            project(NBLK // 2 - 1, j, False)


    @block.scalar
    def _(act):
        def x_hi(k):
            for c in range(KT):
                act.wait_ge(xT_full, KT * k + c + 1)
                nc.scalar.activation(xnT[:, 0, c, :], bank(c), ACT.Copy, scale=X_SCALE).then_inc(xT_saved, 1)

        x_hi(0)
        act.wait_ge(prep, SCALES_READY)
        for n in range(NSPLIT):
            src, sc, rows = split_unit(n)
            nc.scalar.activation(nat16[:, 0, rows, :], src, ACT.Copy, scale=sc).then_inc(hi_ready, 1)
        act.wait_ge(wd_full, 1)
        nc.scalar.activation(woT[:, :, :].rearrange("p k e -> p (k e)"), bank(0), ACT.Copy).then_inc(wd_saved, 1)
        act.wait_ge(wd_full, 2)
        for j in range(HT):
            nc.scalar.activation(wdT32[:, j, :], psum[:, BANK + j * D:BANK + (j + 1) * D], ACT.Copy,
                                 scale=h_inv[:, j:j + 1]).then_inc(wd_saved, 1)
        w_flat = w16[:, :, :].rearrange("p a n -> p (a n)")
        for grp in range(WG):
            act.wait_ge(wt_full, grp + 1)
            nc.scalar.activation(w_flat[:, grp * 8 * P:(grp + 1) * 8 * P], bank(4 + grp % 4).bitcast(F16),
                                 ACT.Copy).then_inc(wt_saved, 1)

        def h_hi(k, j):
            act.wait_ge(pair_used, PAIRS * k + BLK + j + 1)
            nc.scalar.activation(hT[:, 0, j, :], h32[:, j % H_BUFS, :], ACT.Copy).then_inc(hhi_ready, 1)

        def hi_part(k, t):
            act.wait_ge(qk_ready, BLK * k + t + 1)
            if not (isinstance(k, int) and k == 0):
                act.wait_ge(partsT_full, BLK * k)
            nc.scalar.activation(parts[:, t, 0, :], qk_rot[:, t, :], ACT.Copy).then_inc(part_hi, 1)

        def block_a(k, last):
            hi_part(k, 0)
            hi_part(k, 1)
            for j in range(HT):
                act.wait_ge(pair_full, PAIRS * k + BLK + j + 1)
                nc.scalar.activation(silu[:, j % 2, :], bank(PAIR_BANK[BLK + j]), ACT.Silu,
                                     scale=gate_fix[:, j:j + 1]).then_inc(silu_ready, 1)
                if 1 <= j <= BLK:
                    t = j - 1
                    if t == 0 and not (isinstance(k, int) and k == 0):
                        act.wait_ge(staged_out, 16 * N_STAGED * k)
                    act.wait_ge(partsT_full, BLK * k + t + 1)
                    nc.scalar.activation(staged[:, :, :, t * P:(t + 1) * P],
                                         psum[:, 0:2 * BANK].bitcast(BF16)[:, 0:PARTS * 2 * KT * P].rearrange(
                                             "p (a q n) -> p a q n", a=PARTS, q=2 * KT),
                                         ACT.Copy).then_inc(partsT_saved, 1)
                    h_hi(k, j - 1)
                if j >= BLK:
                    h_hi(k, j)
            if not last:
                x_hi(k + 1)

        block_a(0, False)
        with act.Fori(1, NBLK - 1) as k:
            block_a(k, False)
        block_a(NBLK - 1, True)

        act.wait_ge(down_full, BLK * NBLK)
        act.wait_ge(y_ready, BLK * NBLK)
        act.wait_ge(y_out, 16 * NBLK)
        act.wait_ge(staged_out, 16 * N_STAGED * NBLK)

        def step(c, i):
            item = items_before(c)

            def arrived(item):
                act.wait_ge(s2_full, item + 1 + HEAD_ITEMS * SLOTS * i)
                return 4 + item % RING

            h = head_of(c, SAVE_AT)
            if h is not None:
                act.wait_ge(pv_done, TILES * (h + 1 + SLOTS * i))
                nc.scalar.activation(acc_sb[:, :], bank(7), ACT.Copy).then_inc(acc_saved, 1)
            h = head_of(c, STAB_AT)
            if h is not None:
                if h >= 1:
                    act.wait_ge(stab_loaded, 16 * (h + SLOTS * i))
                b = arrived(item)
                nc.scalar.activation(stabT[:, :], bank(b).bitcast(BF16)[0:PARTS * TILES, 0:P], ACT.Copy).then_inc(s2_used, 1)
                item += 1
            h = head_of(c, TURN_AT)
            if h is not None:
                if h >= 1:
                    act.wait_ge(o_ready, h + SLOTS * i)
                b = arrived(item)
                nc.scalar.activation(oT_sb[:, :], bank(b), ACT.Copy).then_inc(s2_used, 1)
                item += 1
            g2 = c - FIRST2
            if 0 <= g2 < N1:
                if g2 >= 2:
                    act.wait_ge(pv_done, g2 - 1 + UNROLL * i)
                for j in range(4):
                    b = arrived(item)
                    nc.scalar.activation(probs[:, g2 % 2, j * BANK:(j + 1) * BANK], bank(b), ACT.Exp,
                                         scale=SCALE).then_inc(s2_used, 1)
                    item += 1

        run_steps(act, step)

        def save_oT(n, j):
            k = 2 * n + j
            act.wait_ge(proj_full, 2 * (k - 1))
            for c in range(KT):
                act.wait_ge(cT_full, KT * k + c + 1)
                nc.scalar.activation(oT[:, j, c, :], bank(2 * j + c), ACT.Copy).then_inc(cT_saved, 1)

        for j in range(2):
            save_oT(1, j)
        with act.Fori(2, NBLK // 2) as n:
            for j in range(2):
                save_oT(n, j)

    @block.gpsimd
    def _(pool):
        pool.wait_ge(ident_loaded, 16)
        nc.gpsimd.tensor_copy(ident16[:, :], ident[:, :]).then_inc(ident16_ready, 1)
        nc.gpsimd.tensor_copy(identh[:, :], ident[:, :]).then_inc(ident16_ready, 1)
        pool.wait_ge(wdown_loaded, 16)
        nc.gpsimd.tensor_copy(nat["d"], nat["di"]).then_inc(down_float, 1)
        pool.wait_ge(prep, MAT_MAX_READY)
        pool.wait_ge(ident16_ready, 2)
        pool.wait_ge(down_float, 1)
        nc.gpsimd.partition_all_reduce(mat_max[:, 1, :], mat_max[:, 0, :], P, RMAX).then_inc(mat_reduced, 1)
        pool.wait_ge(down_ready, 1)
        pool.wait_ge(mat_reduced, 1)
        nc.gpsimd.partition_all_reduce(down_max[:, 1, :], down_max[:, 0, :], P, RMAX).then_inc(mat_reduced, 1)
        pool.wait_ge(prep, LO_MAX_READY)
        pool.wait_ge(mat_reduced, 2)
        nc.gpsimd.partition_all_reduce(lo_max[:, 2, 0:1], lo_max[:, 1, 0:1], P, RMAX).then_inc(lo_bits_ready, 1)

        def qk_sum(k, t):
            pool.wait_ge(rope_ready, BLK * k + t + 1)
            if not (isinstance(k, int) and k == 0):
                pool.wait_ge(rem_ready, BLK * (k - 1) + t + 1)
            nc.gpsimd.tensor_tensor(qk_rot[:, t, :], rot_c[:, t % 2, :], rot_s[:, t % 2, :],
                                    ALU.add).then_inc(qk_ready, 1)

        def lo_part(k, t):
            pool.wait_ge(part_mid, BLK * k + t + 1)
            nc.gpsimd.tensor_tensor(parts[:, t, 2, :], qk_rem[:, t % 2, :], parts[:, t, 1, :],
                                    ALU.subtract).then_inc(parts_ready, 1)

        def h_lo(k, j):
            pool.wait_ge(hhi_ready, HT * k + j + 1)
            nc.gpsimd.tensor_tensor(hT[:, 1, j, :], h32[:, j % H_BUFS, :], hT[:, 0, j, :], ALU.subtract).then_inc(hlo_ready, 1)

        def block_a(k):
            qk_sum(k, 0)
            qk_sum(k, 1)
            lo_part(k, 0)
            qk_sum(k, 2)
            lo_part(k, 1)
            qk_sum(k, 3)
            lo_part(k, 2)
            h_lo(k, 0)
            lo_part(k, 3)
            h_lo(k, 1)
            for j in range(2, HT - 1):
                h_lo(k, j)

        block_a(0)
        with pool.Fori(1, NBLK) as k:
            block_a(k)

        pool.wait_ge(down_full, BLK * NBLK)
        pool.wait_ge(y_ready, BLK * NBLK)
        pool.wait_ge(y_out, 16 * NBLK)
        pool.wait_ge(staged_out, 16 * N_STAGED * NBLK)
        nc.gpsimd.memset(k_op[ROWS:ROWS + 32, :, :], 1.0).then_inc(b_const, 1)
        pool.wait_ge(b_const, 1)
        nc.gpsimd.memset(v_op[:, :, :, DH:DH + 1], 1.0).then_inc(b_const, 1)
        pool.wait_ge(b_const, 2)
        nc.gpsimd.memset(v_op[:, :, :, DH + 1:32], 0.0).then_inc(b_const, 1)
        pool.wait_ge(b_const, 3)
        nc.gpsimd.memset(stab[:, :, :], 0.0).then_inc(b_const, 1)
        pool.wait_ge(b_const, 4)
        nc.gpsimd.memset(zero[:, :], 0.0).then_inc(b_const, 1)
        pool.wait_ge(b_const, 5)

        def split_max(h, first):
            n = 4 * h
            pool.wait_ge(max_ready, h + 1)
            if not first:
                pool.wait_ge(stab_loaded, 16 * h)
            nc.gpsimd.tensor_tensor(stab[:, 0, :], neg_max[:, :], zero[:, :], ALU.add).then_inc(stab_step, 1)
            pool.wait_ge(stab_step, n + 1)
            nc.gpsimd.tensor_tensor(neg_rem[:, :], neg_max[:, :], stab[:, 0, :], ALU.subtract).then_inc(stab_step, 1)
            pool.wait_ge(stab_step, n + 2)
            nc.gpsimd.tensor_tensor(stab[:, 1, :], neg_rem[:, :], zero[:, :], ALU.add).then_inc(stab_step, 1)
            pool.wait_ge(stab_step, n + 3)
            nc.gpsimd.tensor_tensor(stab[:, 2, :], neg_rem[:, :], stab[:, 1, :], ALU.subtract).then_inc(stab_step, 1)

        split_max(0, True)
        with pool.Fori(1, HEADS) as h:
            split_max(h, False)

    @block.vector
    def _(dve):
        def row_stats(k):
            dve.wait_ge(x_loaded, 16 * (k + 1))
            for t in range(BLK):
                ins = nc.vector.bn_stats(stats[:, t, :], x_ln[:, t, :])
            ins.then_inc(ln_step, 1)
            dve.wait_ge(ln_step, LN_STEPS * k + 1)

        def ln_steps(k, n):
            count = [LN_STEPS * k + n]

            def done(ins):
                count[0] = count[0] + 1
                ins.then_inc(ln_step, 1)

            def wait():
                dve.wait_ge(ln_step, count[0])

            return done, wait

        def ln_seed(k):
            done, wait = ln_steps(k, 1)
            for t in range(BLK):
                ins = nc.vector.bn_aggr(mv[:, t, :], stats[:, t, :])
            done(ins)
            wait()
            done(nc.vector.tensor_scalar(ve[:, :], mv[:, :, 1], EPS, None, ALU.add))
            wait()
            done(nc.vector.tensor_scalar(seed[:, :], ve[:, :].bitcast(I32), 1, None, ALU.logical_shift_right))
            wait()
            done(nc.vector.tensor_scalar(rs[:, 0, :].bitcast(I32), seed[:, :], -1.0, float(0x5F3759DF), ALU.mult, ALU.add))
            wait()

        def ln_newton(k, r):
            done, wait = ln_steps(k, 5 + 4 * r)
            done(nc.vector.tensor_tensor(nt_a[:, r, :], rs[:, r, :], rs[:, r, :], ALU.mult))
            wait()
            done(nc.vector.tensor_tensor(nt_b[:, r, :], nt_a[:, r, :], ve[:, :], ALU.mult))
            wait()
            done(nc.vector.tensor_scalar(nt_a[:, r, :], nt_b[:, r, :], -0.5, 1.5, ALU.mult, ALU.add))
            wait()
            done(nc.vector.tensor_tensor(rs[:, r + 1, :], rs[:, r, :], nt_a[:, r, :], ALU.mult))
            wait()

        def normalise(k, first):
            if not first:
                dve.wait_ge(xT_full, KT * k)
            for t in range(BLK):
                ins = nc.vector.tensor_scalar(xn[:, t, :], x_ln[:, t, :], mv[:, t, 0:1], rs[:, 3, t:t + 1],
                                              ALU.subtract, ALU.mult)
            ins.then_inc(xn_ready, 1)

        def x_lo(k, c):
            dve.wait_ge(xT_saved, KT * k + c + 1)
            nc.vector.scalar_tensor_tensor(xnT[:, 1, c, :], bank(c), X_SCALE, xnT[:, 0, c, :], ALU.mult,
                                           ALU.subtract).then_inc(xlo_ready, 1)

        row_stats(0)
        ln_seed(0)
        for r in range(3):
            ln_newton(0, r)
        normalise(0, True)

        count = [0]

        def step_done(ins):
            count[0] += 1
            ins.then_inc(prep, 1)

        def wait_prep():
            dve.wait_ge(prep, count[0])

        def powers(dst_pow, dst_inv, src):
            step_done(nc.vector.tensor_scalar(dst_pow.bitcast(I32), src.bitcast(I32), EXPONENT, None, ALU.bitwise_and))
            wait_prep()
            step_done(nc.vector.tensor_scalar(dst_inv.bitcast(I32), dst_pow.bitcast(I32), -1.0, TWO_EXPONENTS, ALU.mult, ALU.add))

        dve.wait_ge(wqkv_loaded, 16)
        step_done(nc.vector.tensor_reduce(largest[:, 0:NQ], nat["qkv"], AX.X, ALU.max, apply_absolute_value=True))
        for c in range(KT):
            x_lo(0, c)
        dve.wait_ge(wgate_loaded, 16)
        step_done(nc.vector.tensor_reduce(largest[:, NQ:NQ + HT], nat["gi"], AX.X, ALU.max, apply_absolute_value=True))
        dve.wait_ge(wup_loaded, 16)
        step_done(nc.vector.tensor_reduce(largest[:, NQ + HT:NROW], nat["ui"], AX.X, ALU.max, apply_absolute_value=True))
        wait_prep()
        step_done(nc.vector.tensor_reduce(mat_max[:, 0, 0:1], largest[:, 0:2 * D // P], AX.X, ALU.max))
        step_done(nc.vector.tensor_reduce(mat_max[:, 0, 1:2], largest[:, 2 * D // P:NQ], AX.X, ALU.max))
        assert count[0] == MAT_MAX_READY, count
        step_done(nc.vector.tensor_scalar(row_max1[:, :], largest[:, NQ:NROW], 1.0, None, ALU.max))
        wait_prep()
        powers(pow_gu[:, :], inv_gu[:, :], row_max1[:, :])
        wait_prep()
        step_done(nc.vector.tensor_scalar(scale_gu[:, :], inv_gu[:, :], W_SCALE, None, ALU.mult))
        step_done(nc.vector.tensor_scalar(gate_fix[:, :], pow_gu[:, 0:HT], QUANT_SCALE / (W_SCALE * X_SCALE), None, ALU.mult))
        step_done(nc.vector.tensor_scalar(h_fix[:, :], inv_gu[:, 0:HT], QUANT_SCALE * H_SCALE / (W_SCALE * X_SCALE), None,
                                          ALU.mult))
        step_done(nc.vector.tensor_tensor(pow_prod[:, :], pow_gu[:, 0:HT], pow_gu[:, HT:2 * HT], ALU.mult))
        wait_prep()
        step_done(nc.vector.tensor_scalar(h_inv[:, :], pow_prod[:, :], 1.0 / H_SCALE, None, ALU.mult))
        dve.wait_ge(mat_reduced, 1)
        step_done(nc.vector.tensor_scalar(mat_max[:, 2, :], mat_max[:, 1, :], 1e-30, None, ALU.max))
        wait_prep()
        powers(pow_m[:, 0:2], inv_m[:, 0:2], mat_max[:, 2, :])
        wait_prep()
        step_done(nc.vector.tensor_scalar(scale_m[:, 0:2], inv_m[:, 0:2], W_SCALE, None, ALU.mult))
        step_done(nc.vector.tensor_scalar(fix_m[:, 0:2], pow_m[:, 0:2], 1.0 / (W_SCALE * X_SCALE), None, ALU.mult))
        assert count[0] == SCALES_READY, count
        wait_prep()
        for n in range(NSPLIT):
            src, sc, rows = split_unit(n)
            dve.wait_ge(hi_ready, n + 1)
            nc.vector.scalar_tensor_tensor(nat16[:, 1, rows, :], src, sc, nat16[:, 0, rows, :], ALU.mult,
                                           ALU.subtract).then_inc(lo_ready, 1)
        step_done(nc.vector.tensor_reduce(gu_max[:, :], largest[:, NQ:NROW], AX.X, ALU.max))
        wait_prep()
        step_done(nc.vector.tensor_scalar(lo_max[:, 0, 0:1], gu_max[:, :], EXACT_INT, 0.0, ALU.subtract, ALU.max))
        dve.wait_ge(tables_loaded, 32)
        step_done(nc.vector.tensor_scalar(cos_t[:, :, :], cos_t[:, :, :], fix_m[:, 0:1], None, ALU.mult))
        step_done(nc.vector.tensor_scalar(sin_t[:, :, :], sin_t[:, :, :], fix_m[:, 0:1], None, ALU.mult))
        dve.wait_ge(wd_saved, 1 + HT)
        nc.vector.tensor_reduce(down_max[:, 0, :], wdT32, AX.XY, ALU.max, apply_absolute_value=True).then_inc(down_ready, 1)
        dve.wait_ge(mat_reduced, 2)
        step_done(nc.vector.tensor_scalar(down_max[:, 2, :], down_max[:, 1, :], 1e-30, None, ALU.max))
        wait_prep()
        powers(pow_m[:, 2:3], inv_m[:, 2:3], down_max[:, 2, :])
        wait_prep()
        step_done(nc.vector.tensor_scalar(scale_m[:, 2:3], inv_m[:, 2:3], W_SCALE, None, ALU.mult))
        step_done(nc.vector.tensor_scalar(fix_m[:, 2:3], pow_m[:, 2:3], QUANT_SCALE / W_SCALE, None, ALU.mult))
        wait_prep()
        step_done(nc.vector.tensor_scalar(wdT[:, 0], wdT32, scale_m[:, 2:3], None, ALU.mult))
        wait_prep()
        step_done(nc.vector.scalar_tensor_tensor(wdT[:, 1], wdT32, scale_m[:, 2:3], wdT[:, 0], ALU.mult, ALU.subtract))
        assert count[0] == DOWN_SPLIT, count
        wait_prep()
        step_done(nc.vector.tensor_reduce(lo_max[:, 0, 1:2], wdT[:, 1], AX.XY, ALU.max, apply_absolute_value=True))
        wait_prep()
        step_done(nc.vector.tensor_reduce(lo_max[:, 1, 0:1], lo_max[:, 0, :], AX.X, ALU.max))
        assert count[0] == LO_MAX_READY, count

        def rope(k, t):
            dve.wait_ge(pair_full, PAIRS * k + t + 1)
            if t >= 2 or not (isinstance(k, int) and k == 0):
                dve.wait_ge(qk_ready, BLK * k + t - 1)
            G = 2 * H
            a, b = PAIR_BANK[t], PAIR_BANK[t] + 1
            qk = bank(a).rearrange("p (g s f) -> p g s f", g=G, s=2)
            rc = rot_c[:, t % 2, :].rearrange("p (g s f) -> p g s f", g=G, s=2)
            rsn = rot_s[:, t % 2, :].rearrange("p (g s f) -> p g s f", g=G, s=2)
            tile = k * BLK + t
            HF = DH // 2
            cos = cos_t[:, bass.ds(tile, 1), :].rearrange("p a f -> p (a f)")
            sin = sin_t[:, bass.ds(tile, 1), :].rearrange("p a f -> p (a f)")
            for s in range(2):
                nc.vector.tensor_tensor(rc[:, :, s, :], qk[:, :, s, :], cos.unsqueeze(1).to_broadcast([P, G, HF]), ALU.mult)
            for s in range(2):
                ins = nc.vector.tensor_tensor(rsn[:, :, s, :], qk[:, :, 1 - s, :],
                                              sin[:, s * HF:(s + 1) * HF].unsqueeze(1).to_broadcast([P, G, HF]), ALU.mult)
            ins.then_inc(rope_ready, 1)
            nc.vector.tensor_scalar(v_all[:, bass.ds(tile, 1), :, :].rearrange("p a h d -> p (a h d)"), bank(b, D), fix_m[:, 1:2],
                                    None, ALU.mult).then_inc(pair_used, 1)

        def mid_part(k, t):
            if t < 2:
                dve.wait_ge(part_hi, 2 * k + t + 1)
            else:
                dve.wait_ge(qk_ready, BLK * k + t + 1)
                if not (isinstance(k, int) and k == 0):
                    dve.wait_ge(partsT_full, BLK * k)
                nc.vector.tensor_copy(parts[:, t, 0, :], qk_rot[:, t, :]).then_inc(part_hi_v, 1)
                dve.wait_ge(part_hi_v, 2 * k + t - 1)
            if t >= 2 or not (isinstance(k, int) and k == 0):
                dve.wait_ge(parts_ready, BLK * k + t - 1)
            nc.vector.tensor_tensor(qk_rem[:, t % 2, :], qk_rot[:, t, :], parts[:, t, 0, :],
                                    ALU.subtract).then_inc(rem_ready, 1)
            dve.wait_ge(rem_ready, BLK * k + t + 1)
            nc.vector.tensor_copy(parts[:, t, 1, :], qk_rem[:, t % 2, :]).then_inc(part_mid, 1)

        def gate_up(k, j):
            dve.wait_ge(silu_ready, HT * k + j + 1)
            dve.wait_ge(pair_full, PAIRS * k + BLK + j + 1)
            if j >= H_BUFS:
                dve.wait_ge(hlo_ready, HT * k + j - H_BUFS + 1)
            elif not (isinstance(k, int) and k == 0):
                dve.wait_ge(hlo_ready, HT * k)
            nc.vector.scalar_tensor_tensor(h32[:, j % H_BUFS, :], bank(PAIR_BANK[BLK + j] + 1), h_fix[:, j:j + 1], silu[:, j % 2, :],
                                           ALU.mult, ALU.mult).then_inc(pair_used, 1)

        def add_x(k, t):
            dve.wait_ge(down_full, BLK * k + t + 1)
            if t == 0:
                dve.wait_ge(xres_loaded, 16 * (k + 1))
                if not (isinstance(k, int) and k == 0):
                    dve.wait_ge(y_out, 16 * k)
            nc.vector.scalar_tensor_tensor(y_blk[:, t, :], bank(DOWN_BANK[t], D), fix_m[:, 2:3], x_res[:, t, :], ALU.mult,
                                           ALU.add).then_inc(y_ready, 1)

        def block_a(k, left):
            rope(k, 0)
            rope(k, 1)
            mid_part(k, 0)
            rope(k, 2)
            mid_part(k, 1)
            rope(k, 3)
            gate_up(k, 0)
            mid_part(k, 2)
            gate_up(k, 1)
            mid_part(k, 3)
            if isinstance(k, int) and k == 0:
                row_stats(1)
                ln_seed(1)
                for r in range(3):
                    ln_newton(1, r)
            gate_up(k, 2)
            if left >= 1:
                normalise(k + 1, False)
            gate_up(k, 3)
            gate_up(k, 4)
            gate_up(k, HT - 1)
            dve.wait_ge(hhi_ready, HT * (k + 1))
            dve.wait_ge(hlo_ready, HT * (k + 1) - 1)
            nc.vector.tensor_tensor(hT[:, 1, HT - 1, :], h32[:, (HT - 1) % H_BUFS, :], hT[:, 0, HT - 1, :],
                                    ALU.subtract).then_inc(hlo_ready, 1)
            if left >= 1:
                for c in range(KT):
                    x_lo(k + 1, c)
            if left >= 2:
                row_stats(k + 2)
            for t in range(PREFIX):
                add_x(k, t)
            if left >= 2:
                ln_seed(k + 2)
                ln_newton(k + 2, 0)
            for t in range(PREFIX, BLK):
                add_x(k, t)
            if left >= 2:
                ln_newton(k + 2, 1)
                ln_newton(k + 2, 2)

        dve.wait_ge(wt_saved, WG)
        block_a(0, 2)
        with dve.Fori(1, NBLK - 2) as k:
            block_a(k, 2)
        block_a(NBLK - 2, 1)
        block_a(NBLK - 1, 0)

        dve.wait_ge(b_const, 5)

        def gather(n, j, first):
            k = 2 * n + j
            if not first:
                dve.wait_ge(cT_full, KT * (k - 1))
            nc.vector.tensor_scalar(o_blk[:, j, :, :], o_all[:, bass.ds(k * BLK, BLK), :, :].rearrange("p t h d -> p t (h d)"),
                                    1.0, None, ALU.mult).then_inc(c_gathered, 1)

        def add_y(n, j, first):
            k = 2 * n + j
            dve.wait_ge(yin_loaded[j], 16 * (n + 1))
            if not first:
                dve.wait_ge(res_out[j], 16 * n)
            for u in range(2):
                dve.wait_ge(proj_full, 2 * k + u + 1)
                nc.vector.tensor_tensor(res[:, j, 2 * u:2 * u + 2, :], bank(4 + 2 * j + u).rearrange("p (t d) -> p t d", t=2),
                                        y_in[:, j, 2 * u:2 * u + 2, :], ALU.add).then_inc(res_ready, 1)

        def save_first():
            for j in range(2):
                for c in range(KT):
                    dve.wait_ge(cT_full, KT * j + c + 1)
                    nc.vector.tensor_scalar(oT[:, j, c, :], bank(2 * j + c), 1.0, None, ALU.mult).then_inc(cT_saved, 1)

        def step(c, i):
            hl, t = divmod(c, TILES)
            h = head_of(c, TILES)
            if h is not None:
                dve.wait_ge(s1_used, 2 * TILES * (h + 1 + SLOTS * i))
                if h >= 1:
                    dve.wait_ge(stab_step, 4 * (h + SLOTS * i))
                nc.vector.tensor_reduce(neg_max[:, :], row_max[:, h % 2, :, :], AX.X, ALU.max, negate=True).then_inc(max_ready, 1)
            h = head_of(c, VCOPY_AT)
            if h is not None:
                if h >= 2:
                    dve.wait_ge(pv_done, TILES * (h - 1 + SLOTS * i))
                hh = h + SLOTS * i
                src = v_all[:, bass.ds(sequence_of(hh) * TILES, TILES), bass.ds(hh & (H - 1), 1), :].rearrange("p t a d -> p t (a d)")
                nc.vector.tensor_scalar(v_op[:, h % 2, :, 0:DH], src, 1.0, None, ALU.mult).then_inc(v_ready, 1)
            h = head_of(c, NORM_AT)
            if h is not None:
                g = TILES * h + TURN_AT
                dve.wait_ge(s2_used, items_before(g) + 1 + HEAD_ITEMS * SLOTS * i)
                turned = oT_sb[:, :].rearrange("p (n j d) -> p j n d", n=4, j=4)
                if h >= 1:
                    dve.wait_ge(o_ready, h + SLOTS * i)
                nc.vector.reciprocal(inv_sum[:, :, :], turned[:, :, :, DH]).then_inc(sum_inv, 1)
                dve.wait_ge(sum_inv, h + 1 + SLOTS * i)
                hh = h + SLOTS * i
                dst = o_all[:, bass.ds(sequence_of(hh) * TILES, TILES), bass.ds(hh & (H - 1), 1), :].rearrange(
                    "p (j n) a d -> p j n (a d)", j=4)
                nc.vector.tensor_tensor(dst, turned[:, :, :, 0:DH], inv_sum[:, :, :].unsqueeze(3).to_broadcast([P, 4, 4, DH]),
                                        ALU.mult).then_inc(o_ready, 1)
            if c < N1:
                for half in range(2):
                    dve.wait_ge(s1_full, 2 * c + half + 1 + 2 * UNROLL * i)
                    nc.vector.tensor_reduce(row_max[:, hl % 2, t, half:half + 1], psum[:, 2 * half * BANK:(2 * half + 2) * BANK],
                                            AX.X, ALU.max).then_inc(s1_used, 1)

            if c == FIRST_C:
                dve.wait_ge(o_ready, H)
                for j in range(2):
                    gather(0, j, True)
                save_first()

        run_steps(dve, step)

        dve.wait_ge(o_ready, HEADS)
        for j in range(2):
            gather(1, j, False)
            add_y(0, j, True)
        with dve.Fori(1, NBLK // 2 - 1) as n:
            for j in range(2):
                gather(n + 1, j, False)
                add_y(n, j, False)
        for j in range(2):
            add_y(NBLK // 2 - 1, j, False)

    keep.close()


def kernel(**inputs):
    import numpy as np
    import concourse.bacc as bacc
    from concourse.bass_utils import run_bass_kernel_spmd

    xs = np.ascontiguousarray(inputs["L0_attn_x"])
    nb, L, D = xs.shape
    n_tok = nb * L
    half = DH // 2
    inv_freq = (np.float32(1.0) / np.power(np.float32(10000.0), np.arange(half, dtype=np.float32) / np.float32(half))).astype(np.float32)
    ang = np.arange(L, dtype=np.float32)[:, None] * inv_freq[None, :]
    cos, sin = np.cos(ang).astype(np.float32), np.sin(ang).astype(np.float32)
    cos = np.tile(cos, (nb, 1)).reshape(n_tok // P, P, half).transpose(1, 0, 2)
    sin = np.tile(np.concatenate([-sin, sin], axis=1), (nb, 1)).reshape(n_tok // P, P, DH).transpose(1, 0, 2)

    arrays = {
        "in_x": xs.reshape(n_tok, D),
        "in_w_qkv": np.ascontiguousarray(inputs["L0_attn_w_qkv"]),
        "in_w_out": np.ascontiguousarray(inputs["L0_attn_w_out"]),
        "in_w_gate": np.ascontiguousarray(inputs["L0_ffn_w_gate"]),
        "in_w_up": np.ascontiguousarray(inputs["L0_ffn_w_up"]),
        "in_w_down": np.ascontiguousarray(inputs["L0_ffn_w_down"]),
        "in_cos": np.ascontiguousarray(cos),
        "in_sin": np.ascontiguousarray(sin),
        "in_ident": np.eye(P, dtype=np.float32),
    }
    nc = bacc.Bacc("TRN2", target_bir_lowering=False, num_devices=1)
    ins = [nc.dram_tensor(n, a.shape, mybir.dt.from_np(a.dtype), kind="ExternalInput").ap() for n, a in arrays.items()]
    out = nc.dram_tensor("out_y", (n_tok, D), F32, kind="ExternalOutput").ap()
    y_dram = nc.dram_tensor("y_dram", (n_tok, D), F32, kind="Internal").ap()
    qk_dram = nc.dram_tensor("qk_dram", (2, PARTS, D, n_tok), BF16, kind="Internal").ap()
    layer_program(nc, *ins, out, y_dram, qk_dram)
    r = run_bass_kernel_spmd(nc, [arrays], core_ids=[0])
    return r.results[0]["out_y"].reshape(nb, L, D)
```
